# Optimizing a Trainium2 kernel written in Bass

```python
import numpy as np
import jax
import jax.numpy as jnp

def _softmax(x, axis=-1):
    return jax.nn.softmax(x, axis=axis)

def _gelu(x):
    return jax.nn.gelu(x, approximate=True)

def _silu(x):
    return jax.nn.silu(x)

def _sigmoid(x):
    return jax.nn.sigmoid(x)

def _layernorm(x, axis=-1, eps=1e-05):
    m = jnp.mean(x, axis=axis, keepdims=True)
    v = jnp.var(x, axis=axis, keepdims=True)
    return (x - m) / jnp.sqrt(v + eps)

def _scatter_add(tgt, idx, src, axis=0):
    return tgt.at[idx].add(src)

def _segment_sum(src, seg, n):
    return jax.ops.segment_sum(src, seg, n)
kernel_name = 'mk_gnn_resnorm_d2_gnn_r32_e8f6f0'

def setup_inputs(seed: int=0):
    np.random.seed(seed)
    _w = jnp.asarray

    def _rec_inputs():
        import jax
        import jax.numpy as jnp
        _gk = jax.random.key(seed)
        x = -0.0002928 + 1 * jax.random.normal(jax.random.fold_in(_gk, 1), (512, 256), jnp.float32)
        src = jax.random.randint(jax.random.fold_in(_gk, 2), (16384,), 0, 512, jnp.int32)
        dst = jnp.minimum((512 * jax.random.uniform(jax.random.fold_in(_gk, 3), (16384,)) ** 2.0).astype(jnp.int32), 16383)
        _o = jnp.argsort(dst, stable=True)
        src = src[_o]
        dst = dst[_o]
        edge_attr_512 = -9.86303e-05 + 0.999976 * jax.random.normal(jax.random.fold_in(_gk, 11), (16384, 512), jnp.float32)
        return (x, src, dst, edge_attr_512)
    x, src, dst, edge_attr_512 = _rec_inputs()

    def _L0_gnn_setup():
        import jax, jax.numpy as jnp
        import numpy as np
        N_NODES = 512
        LN_EPS = 1e-05
        SCALE = 30.0

        def _layer_norm(x, g, b):
            mu = jnp.mean(x, axis=-1, keepdims=True)
            var = jnp.mean(jnp.square(x - mu), axis=-1, keepdims=True)
            return (x - mu) * jax.lax.rsqrt(var + LN_EPS) * g + b
        key = jax.random.key(seed)
        ks = jax.random.split(key, 20)
        N, E, H, EIN, D = (512, 16384, 256, 512, 1024)

        def lin(k, fan_in, fan_out):
            k1, k2 = jax.random.split(k)
            lim = 1.0 / np.sqrt(fan_in)
            w = jax.random.uniform(k1, (fan_in, fan_out), jnp.float32, -lim, lim)
            b = jax.random.uniform(k2, (fan_out,), jnp.float32, -lim, lim)
            return (w, b)
        h_V = jax.random.normal(ks[0], (N, H), jnp.float32)
        h_E = jax.random.normal(ks[1], (E, EIN), jnp.float32)
        edge_idx = jax.random.randint(ks[2], (2, E), 0, N, jnp.int64)
        m0_w, m0_b = lin(ks[3], EIN, H)
        m1_w, m1_b = lin(ks[4], H, H)
        m2_w, m2_b = lin(ks[5], H, H)
        d0_w, d0_b = lin(ks[6], H, D)
        d1_w, d1_b = lin(ks[7], D, D)
        d2_w, d2_b = lin(ks[8], D, H)
        ln1_g = jnp.ones((H,), jnp.float32)
        ln1_b = jnp.zeros((H,), jnp.float32)
        ln2_g = jnp.ones((H,), jnp.float32)
        ln2_b = jnp.zeros((H,), jnp.float32)
        return dict(h_V=h_V, h_E=h_E, edge_idx=edge_idx, m0_w=m0_w, m0_b=m0_b, m1_w=m1_w, m1_b=m1_b, m2_w=m2_w, m2_b=m2_b, d0_w=d0_w, d0_b=d0_b, d1_w=d1_w, d1_b=d1_b, d2_w=d2_w, d2_b=d2_b, ln1_g=ln1_g, ln1_b=ln1_b, ln2_g=ln2_g, ln2_b=ln2_b)
    _L0_gnn_all = _L0_gnn_setup()
    _L0_gnn_in = {k: v for k, v in _L0_gnn_all.items() if k in ('m0_w', 'm0_b', 'm1_w', 'm1_b', 'm2_w', 'm2_b', 'd0_w', 'd0_b', 'd1_w', 'd1_b', 'd2_w', 'd2_b', 'ln1_g', 'ln1_b', 'ln2_g', 'ln2_b')}
    del _L0_gnn_all

    def _L1_gnn_setup():
        import jax, jax.numpy as jnp
        import numpy as np
        N_NODES = 3125
        N_EDGES = 9375
        D_MODEL = 256
        N_HEADS = 8
        D_HEAD = D_MODEL // N_HEADS

        def _layernorm(x, w, b, eps=1e-05):
            mu = jnp.mean(x, axis=-1, keepdims=True)
            var = jnp.var(x, axis=-1, keepdims=True)
            return (x - mu) * jax.lax.rsqrt(var + eps) * w + b
        key = jax.random.key(seed)
        ks = jax.random.split(key, 16)
        d, h = (D_MODEL, D_MODEL)
        s = 1.0 / np.sqrt(d)
        inp = {'x': jax.random.normal(ks[0], (N_NODES, d), dtype=jnp.float32), 'edge_index': jax.random.randint(ks[1], (2, N_EDGES), 0, N_NODES, dtype=jnp.int64), 'Wq': jax.random.normal(ks[2], (d, d), dtype=jnp.float32) * s, 'Wk': jax.random.normal(ks[3], (d, d), dtype=jnp.float32) * s, 'Wv': jax.random.normal(ks[4], (d, d), dtype=jnp.float32) * s, 'O_w': jax.random.normal(ks[5], (d, d), dtype=jnp.float32) * s, 'O_b': jnp.zeros((d,), dtype=jnp.float32), 'ln1_w': jnp.ones((d,), dtype=jnp.float32), 'ln1_b': jnp.zeros((d,), dtype=jnp.float32), 'f1_w': jax.random.normal(ks[6], (d, 2 * d), dtype=jnp.float32) * s, 'f1_b': jnp.zeros((2 * d,), dtype=jnp.float32), 'f2_w': jax.random.normal(ks[7], (2 * d, d), dtype=jnp.float32) / np.sqrt(2 * d), 'f2_b': jnp.zeros((d,), dtype=jnp.float32), 'ln2_w': jnp.ones((d,), dtype=jnp.float32), 'ln2_b': jnp.zeros((d,), dtype=jnp.float32), 'gru_w_ih': jax.random.normal(ks[8], (d, 3 * h), dtype=jnp.float32) * s, 'gru_w_hh': jax.random.normal(ks[9], (h, 3 * h), dtype=jnp.float32) * s, 'gru_b_ih': jnp.zeros((3 * h,), dtype=jnp.float32), 'gru_b_hh': jnp.zeros((3 * h,), dtype=jnp.float32)}
        return inp
    _L1_gnn_all = _L1_gnn_setup()
    _L1_gnn_in = {k: v for k, v in _L1_gnn_all.items() if k in ('Wq', 'Wk', 'Wv', 'O_w', 'O_b', 'ln1_w', 'ln1_b', 'f1_w', 'f1_b', 'f2_w', 'f2_b', 'ln2_w', 'ln2_b', 'gru_w_ih', 'gru_w_hh', 'gru_b_ih', 'gru_b_hh')}
    del _L1_gnn_all
    return {'x': x, 'src': src, 'dst': dst, 'edge_attr_512': edge_attr_512, 'L0_gnn_m0_w': _L0_gnn_in['m0_w'], 'L0_gnn_m0_b': _L0_gnn_in['m0_b'], 'L0_gnn_m1_w': _L0_gnn_in['m1_w'], 'L0_gnn_m1_b': _L0_gnn_in['m1_b'], 'L0_gnn_m2_w': _L0_gnn_in['m2_w'], 'L0_gnn_m2_b': _L0_gnn_in['m2_b'], 'L0_gnn_d0_w': _L0_gnn_in['d0_w'], 'L0_gnn_d0_b': _L0_gnn_in['d0_b'], 'L0_gnn_d1_w': _L0_gnn_in['d1_w'], 'L0_gnn_d1_b': _L0_gnn_in['d1_b'], 'L0_gnn_d2_w': _L0_gnn_in['d2_w'], 'L0_gnn_d2_b': _L0_gnn_in['d2_b'], 'L0_gnn_ln1_g': _L0_gnn_in['ln1_g'], 'L0_gnn_ln1_b': _L0_gnn_in['ln1_b'], 'L0_gnn_ln2_g': _L0_gnn_in['ln2_g'], 'L0_gnn_ln2_b': _L0_gnn_in['ln2_b'], 'L1_gnn_Wq': _L1_gnn_in['Wq'], 'L1_gnn_Wk': _L1_gnn_in['Wk'], 'L1_gnn_Wv': _L1_gnn_in['Wv'], 'L1_gnn_O_w': _L1_gnn_in['O_w'], 'L1_gnn_O_b': _L1_gnn_in['O_b'], 'L1_gnn_ln1_w': _L1_gnn_in['ln1_w'], 'L1_gnn_ln1_b': _L1_gnn_in['ln1_b'], 'L1_gnn_f1_w': _L1_gnn_in['f1_w'], 'L1_gnn_f1_b': _L1_gnn_in['f1_b'], 'L1_gnn_f2_w': _L1_gnn_in['f2_w'], 'L1_gnn_f2_b': _L1_gnn_in['f2_b'], 'L1_gnn_ln2_w': _L1_gnn_in['ln2_w'], 'L1_gnn_ln2_b': _L1_gnn_in['ln2_b'], 'L1_gnn_gru_w_ih': _L1_gnn_in['gru_w_ih'], 'L1_gnn_gru_w_hh': _L1_gnn_in['gru_w_hh'], 'L1_gnn_gru_b_ih': _L1_gnn_in['gru_b_ih'], 'L1_gnn_gru_b_hh': _L1_gnn_in['gru_b_hh']}

def reference(x, src, dst, edge_attr_512, L0_gnn_m0_w, L0_gnn_m0_b, L0_gnn_m1_w, L0_gnn_m1_b, L0_gnn_m2_w, L0_gnn_m2_b, L0_gnn_d0_w, L0_gnn_d0_b, L0_gnn_d1_w, L0_gnn_d1_b, L0_gnn_d2_w, L0_gnn_d2_b, L0_gnn_ln1_g, L0_gnn_ln1_b, L0_gnn_ln2_g, L0_gnn_ln2_b, L1_gnn_Wq, L1_gnn_Wk, L1_gnn_Wv, L1_gnn_O_w, L1_gnn_O_b, L1_gnn_ln1_w, L1_gnn_ln1_b, L1_gnn_f1_w, L1_gnn_f1_b, L1_gnn_f2_w, L1_gnn_f2_b, L1_gnn_ln2_w, L1_gnn_ln2_b, L1_gnn_gru_w_ih, L1_gnn_gru_w_hh, L1_gnn_gru_b_ih, L1_gnn_gru_b_hh):
    import jax
    import jax.numpy as jnp

    def _L0_gnn_ref(h_V, h_E, edge_idx, m0_w, m0_b, m1_w, m1_b, m2_w, m2_b, d0_w, d0_b, d1_w, d1_b, d2_w, d2_b, ln1_g, ln1_b, ln2_g, ln2_b):
        import jax, jax.numpy as jnp
        import numpy as np
        N_NODES = 512
        LN_EPS = 1e-05
        SCALE = 30.0

        def _layer_norm(x, g, b):
            mu = jnp.mean(x, axis=-1, keepdims=True)
            var = jnp.mean(jnp.square(x - mu), axis=-1, keepdims=True)
            return (x - mu) * jax.lax.rsqrt(var + LN_EPS) * g + b
        gelu = lambda x: jax.nn.gelu(x, approximate=False)
        src_idx = edge_idx[0]
        m = gelu(h_E @ m0_w + m0_b)
        m = gelu(m @ m1_w + m1_b)
        m = gelu(m @ m2_w + m2_b)
        dh = jax.ops.segment_sum(m, src_idx, num_segments=N_NODES) / SCALE
        h = _layer_norm(h_V + dh, ln1_g, ln1_b)
        d = gelu(h @ d0_w + d0_b)
        d = gelu(d @ d1_w + d1_b)
        d = d @ d2_w + d2_b
        return _layer_norm(h + d, ln2_g, ln2_b)

    def _L1_gnn_ref(x, edge_index, Wq, Wk, Wv, O_w, O_b, ln1_w, ln1_b, f1_w, f1_b, f2_w, f2_b, ln2_w, ln2_b, gru_w_ih, gru_w_hh, gru_b_ih, gru_b_hh):
        import jax, jax.numpy as jnp
        import numpy as np
        N_NODES = 3125
        N_EDGES = 9375
        D_MODEL = 256
        N_HEADS = 8
        D_HEAD = D_MODEL // N_HEADS

        def _layernorm(x, w, b, eps=1e-05):
            mu = jnp.mean(x, axis=-1, keepdims=True)
            var = jnp.var(x, axis=-1, keepdims=True)
            return (x - mu) * jax.lax.rsqrt(var + eps) * w + b
        N = x.shape[0]
        H, D = (N_HEADS, D_HEAD)
        Q = (x @ Wq).reshape(N, H, D)
        K = (x @ Wk).reshape(N, H, D)
        V = (x @ Wv).reshape(N, H, D)
        score = jnp.einsum('nhd,ngd->nhg', Q, K) / np.sqrt(D)
        score = jax.nn.softmax(score, axis=-1)
        x1 = jnp.einsum('nhg,ngd->nhd', score, V).reshape(N, H * D)
        src, dst = (edge_index[0], edge_index[1])
        msg = x1[dst] * x1[src]
        attn_out = jax.ops.segment_sum(msg, dst, num_segments=N)
        h = attn_out @ O_w + O_b
        h = x + h
        h = _layernorm(h, ln1_w, ln1_b)
        ffn = jax.nn.relu(h @ f1_w + f1_b) @ f2_w + f2_b
        h = _layernorm(h + ffn, ln2_w, ln2_b)
        gi = h @ gru_w_ih + gru_b_ih
        gh = h @ gru_w_hh + gru_b_hh
        gi_r, gi_z, gi_n = jnp.split(gi, 3, axis=-1)
        gh_r, gh_z, gh_n = jnp.split(gh, 3, axis=-1)
        r = jax.nn.sigmoid(gi_r + gh_r)
        z = jax.nn.sigmoid(gi_z + gh_z)
        n = jnp.tanh(gi_n + r * gh_n)
        return (1.0 - z) * n + z * h
    edge_index = jnp.stack([src, dst])
    x = _layernorm(x + _L0_gnn_ref(x, edge_attr_512, edge_index, L0_gnn_m0_w, L0_gnn_m0_b, L0_gnn_m1_w, L0_gnn_m1_b, L0_gnn_m2_w, L0_gnn_m2_b, L0_gnn_d0_w, L0_gnn_d0_b, L0_gnn_d1_w, L0_gnn_d1_b, L0_gnn_d2_w, L0_gnn_d2_b, L0_gnn_ln1_g, L0_gnn_ln1_b, L0_gnn_ln2_g, L0_gnn_ln2_b), axis=-1)
    x = _layernorm(x + _L1_gnn_ref(x, edge_index, L1_gnn_Wq, L1_gnn_Wk, L1_gnn_Wv, L1_gnn_O_w, L1_gnn_O_b, L1_gnn_ln1_w, L1_gnn_ln1_b, L1_gnn_f1_w, L1_gnn_f1_b, L1_gnn_f2_w, L1_gnn_f2_b, L1_gnn_ln2_w, L1_gnn_ln2_b, L1_gnn_gru_w_ih, L1_gnn_gru_w_hh, L1_gnn_gru_b_ih, L1_gnn_gru_b_hh), axis=-1)
    return x

_drawn_inputs = setup_inputs


def setup_inputs(seed=0):
    import zlib

    import numpy as np

    out = dict(_drawn_inputs(seed))
    spreads = {'L0_gnn_ln1_g': (1.0, 0.2),
     'L0_gnn_ln1_b': (0.0, 0.1),
     'L0_gnn_ln2_g': (1.0, 0.2),
     'L0_gnn_ln2_b': (0.0, 0.1),
     'L1_gnn_O_b': (0.0, 0.456),
     'L1_gnn_ln1_w': (1.0, 0.2),
     'L1_gnn_ln1_b': (0.0, 0.1),
     'L1_gnn_f1_b': (0.0, 0.1),
     'L1_gnn_f2_b': (0.0, 0.1),
     'L1_gnn_ln2_w': (1.0, 0.2),
     'L1_gnn_ln2_b': (0.0, 0.1),
     'L1_gnn_gru_b_ih': (0.0, 0.1),
     'L1_gnn_gru_b_hh': (0.0, 0.35)}
    factors = {'edge_attr_512': 8.0,
     'L0_gnn_m0_w': 8.0,
     'L0_gnn_m0_b': 64.0,
     'L0_gnn_m1_w': 5.062,
     'L0_gnn_m1_b': 64.0,
     'L0_gnn_m2_w': 4.636,
     'L0_gnn_m2_b': 123.085,
     'L0_gnn_d0_b': 8.0,
     'L0_gnn_d1_b': 8.0,
     'L0_gnn_d2_b': 3.146}
    for name, (base, spread) in spreads.items():
        noise = np.random.default_rng([zlib.crc32(name.encode()), seed]).standard_normal(out[name].shape)
        drawn = base * np.exp(spread * noise) if base else spread * noise
        out[name] = jnp.asarray(drawn.astype(out[name].dtype))
    for name, factor in factors.items():
        out[name] = (out[name] * factor).astype(out[name].dtype)
    return out
```

```python
from contextlib import ExitStack

import concourse.bass as bass
from concourse import mybir

F32 = mybir.dt.float32
F32R = mybir.dt.float32r
BF16 = mybir.dt.bfloat16
FP16 = mybir.dt.float16
I32 = mybir.dt.int32
ALU = mybir.AluOpType
ACT = mybir.ActivationFunctionType
AX_X = mybir.AxisListType.X

P = 128
N = 512
H = 256
E = 16384
EIN = 512
D = 1024
HEADS = 8
DH = H // HEADS
BLK = 512
TB = BLK // P
NBLK = E // BLK
KE = EIN // P
KH = H // P
KD = D // P
NC = N // P
LN_EPS = 1e-5
WINDOW = 4
PACK_BITS = 12
RSQRT_SEED = 0x5F3759DF

COLS = {}
_at = 0
for _name, _n in (("m0_b", KH), ("m1_b", KH), ("ln1_g", KH), ("ln1_b", KH), ("d0_b", KD), ("d1_b", KD),
                  ("t_ln1_w", KH), ("t_ln1_b", KH), ("f1_b", 4), ("t_ln2_w", KH), ("t_ln2_b", KH)):
    COLS[_name] = (_at, _n)
    _at += _n
NCOLS = _at
ROWS = {}
_at = 0
for _name, _n in (("ln1_g", H), ("ln1_b", H), ("d2_b", H), ("ln2_g", H), ("ln2_b", H), ("O_b", H),
                  ("t_ln1_w", H), ("t_ln1_b", H), ("f2_b", H), ("t_ln2_w", H), ("t_ln2_b", H),
                  ("b_ih", 3 * H), ("b_hh", 3 * H)):
    ROWS[_name] = (_at, _n)
    _at += _n
NROWS = _at


def gnn_kernel(nc, x_rows_d, edges_d, src_d, dst_d, w0_d, w1_d, w2_d, m2b_d, cols_d, rows_d, d0_d, d1_d, d2_d,
               wqk_d, wv_d, wo_d, f1_d, f2_d, wih_d, whh_d, out_d):
    ctx = ExitStack()
    with ctx:
        mem = [ctx]

        def sb(name, shape, dt=F32):
            return mem[0].enter_context(nc.sbuf_tensor(name, shape, dt))

        def sem(name):
            return ctx.enter_context(nc.semaphore(name))

        x_rows = sb("x_rows", [P, NC, H])
        cols = sb("cols", [P, NCOLS])
        d0_w = sb("d0_w", [P, KH, D])
        d1_w = sb("d1_w", [P, KD, D])
        count = sb("count", [P, NC, N])
        ident = sb("ident", [P, P])

        edge_mem = ExitStack()
        mem[0] = edge_mem
        w_raw = sb("w_raw", [P, (KE + 2 * KH) * H])
        w_hi = sb("w_hi", [P, (KE + 2 * KH) * H], F32R)
        w_lo = sb("w_lo", [P, (KE + 2 * KH) * H], F32R)
        m2b = sb("m2b", [P, 2, H])
        x_raw = sb("x_raw", [P, 2, KE, BLK])
        x_hi = sb("x_hi", [P, 2, KE, BLK], F32R)
        x_lo = sb("x_lo", [P, 2, KE, BLK], F32R)
        m0 = sb("m0", [P, KH, BLK])
        m0_hi = sb("m0_hi", [P, KH, BLK], F32R)
        m0_lo = sb("m0_lo", [P, KH, BLK], F32R)
        m1 = sb("m1", [P, KH, BLK])
        m1_hi = sb("m1_hi", [P, KH, BLK], F32R)
        m1_lo = sb("m1_lo", [P, KH, BLK], F32R)
        m2_in = sb("m2_in", [P, 2, 2 * H])
        m2 = sb("m2", [P, 2, 2 * H])
        m2_hi = sb("m2_hi", [P, 2, 2 * H], F32R)
        m2_lo = sb("m2_lo", [P, 2, 2 * H], F32R)
        src_hot = sb("src_hot", [P, 2, TB, N], F32R)
        dst_hot = sb("dst_hot", [P, 2, TB, N], BF16)
        pack_hot = sb("pack_hot", [P, 2, TB, 2 * P], BF16)
        iota_i = sb("iota_i", [P, N], I32)
        iota = sb("iota", [P, N], FP16)
        src_i = sb("src_i", [P, E // P], I32)
        dst_i = sb("dst_i", [P, E // P], I32)
        src_f = sb("src_f", [P, E // P])
        dst_f = sb("dst_f", [P, E // P])
        src_far = sb("src_far", [P, E // P])
        src_in = sb("src_in", [P, E // P])
        src_unit = sb("src_unit", [P, E // P])
        packed = w_raw[:, 0:2 * N].bitcast(I32).rearrange("p (r n) -> p r n", r=2)
        part = w_raw[:, 2 * N:4 * N].bitcast(I32).rearrange("p (r n) -> p r n", r=2)
        edge_mem.close()

        node_mem = ExitStack()
        mem[0] = node_mem
        d2_w = sb("d2_w", [P, KD, H])
        wqk = sb("wqk", [P, KH, 2 * H])
        wv = sb("wv", [P, KH, H])
        wo = sb("wo", [P, KH, H])
        f1_w = sb("f1_w", [P, KH, 2 * H])
        f2_w = sb("f2_w", [P, 4, H])
        w_ih = sb("w_ih", [P, KH, 3 * H])
        w_hh = sb("w_hh", [P, KH, 3 * H])
        rows = sb("rows", [P, NROWS])
        sum_T = sb("sum_T", [P, KH, N])
        res = sb("res", [P, NC, H])
        hat = sb("hat", [P, NC, H])
        stats = sb("stats", [P, NC, 6])
        mean_var = sb("mean_var", [P, NC, 2])
        var = sb("var", [P, NC])
        half_var = sb("half_var", [P, NC])
        rstd = sb("rstd", [P, NC])
        sq = sb("sq", [P, NC])
        h_rows = sb("h_rows", [P, NC, H])
        skip = sb("skip", [P, NC, H])
        skip2 = sb("skip2", [P, NC, H])
        xp = sb("xp", [P, NC, H])
        act_T = sb("act_T", [P, KH, N])
        d0_T = sb("d0_T", [P, KD, N])
        d1_T = sb("d1_T", [P, KD, N])
        qk_rows = sb("qk_rows", [P, NC, 2 * H])
        v_rows = sb("v_rows", [P, NC, H])
        probs = sb("probs", [P, NC, HEADS, HEADS])
        top = sb("top", [P, NC * HEADS])
        total = sb("total", [P, NC * HEADS])
        x1 = sb("x1", [P, NC, H])
        w_rz = sb("w_rz", [P, KH, 2 * H])
        b_rz = sb("b_rz", [P, 2 * H])
        b_n = sb("b_n", [P, 2 * H])
        rz = d0_T[:, 0:4]
        gn = d0_T[:, 4:8]
        cand = d1_T[:, 0:2].rearrange("p a (b f) -> p (a b) f", b=2)
        f1_T = d1_T[:, 4:8]
        prod = d0_T[:].rearrange("p (b k) n -> p b (k n)", b=2)
        node_mem.close()
        mem[0] = ctx

        ps = ctx.enter_context(nc.psum_tensor("ps", [P, 8, 512], F32))
        SUM, CNT = 4, 6

        def rows2(bank):
            return ps[:, bank:bank + 2, :].rearrange("p b (c f) -> p (b c) f", c=2)

        def col(name, i):
            at, _ = COLS[name]
            return cols[:, at + i:at + i + 1]

        def row(name, lo=0, n=None):
            at, size = ROWS[name]
            return rows[:, at + lo:at + lo + (n or size)]

        def row_all(name):
            return row(name).rearrange("p (a f) -> p a f", a=1).to_broadcast([P, NC, H])

        x_loaded = [sem("x_loaded0"), sem("x_loaded1")]
        w_loaded, m2b_loaded, idx_loaded = sem("w_loaded"), sem("m2b_loaded"), sem("idx_loaded")
        cols_loaded, early_loaded, late_loaded = sem("cols_loaded"), sem("early_loaded"), sem("late_loaded")
        iota_ready, iota_cast = sem("iota_ready"), sem("iota_cast")
        ident_zero, ident_ready = sem("ident_zero"), sem("ident_ready")
        w_hi_done, w_split = sem("w_hi_done"), sem("w_split")
        idx_step = sem("idx_step")
        x_hi_done, x_lo_done = sem("x_hi_done"), sem("x_lo_done")
        l0_done, l1_done, l2_done = sem("l0_done"), sem("l1_done"), sem("l2_done")
        gelu0, gelu1, gelu2 = sem("gelu0"), sem("gelu1"), sem("gelu2")
        lo0_done, lo1_done, lo2_done = sem("lo0_done"), sem("lo1_done"), sem("lo2_done")
        m2_biased = sem("m2_biased")
        hot_ready, tile_summed = sem("hot_ready"), sem("tile_summed")
        count_out, count_step = sem("count_out"), sem("count_step")
        sum_scaled, sum_turned = sem("sum_scaled"), sem("sum_turned")
        hat_ready, hat_turned, act_ready = sem("hat_ready"), sem("hat_turned"), sem("act_ready")
        skip_ready = sem("skip_ready")
        d0_done, d0_gelu, d1_done, d1_gelu, d2_done = (sem(n) for n in ("d0_done", "d0_gelu", "d1_done", "d1_gelu", "d2_done"))
        qkv_done, qkv_out = sem("qkv_done"), sem("qkv_out")
        scores_ready, exp_done = sem("scores_ready"), sem("exp_done")
        x1_ready, gathered = sem("x1_ready"), sem("gathered")
        o_done, f1_done, f1_relu, f2_done = sem("o_done"), sem("f1_done"), sem("f1_relu"), sem("f2_done")
        gru_done, rz_ready, rz_sig = sem("gru_done"), sem("rz_ready"), sem("rz_sig")
        cand_ready, cand_tanh = sem("cand_ready"), sem("cand_tanh")
        out_ready, out_stored = sem("out_ready"), sem("out_stored")
        dve_step = sem("dve_step")

        block = ctx.enter_context(nc.Block())

        def wait(eng, s, value):
            if not isinstance(value, int) or value > 0:
                eng.wait_ge(s, value)

        LEAD = 2
        ROUNDS = (NBLK - LEAD - 2) // WINDOW

        class Iteration:
            def __init__(self, b, rnd=None):
                self.b, self.rnd = b, rnd
                self.phase, self.par = b % WINDOW, b % 2

            def count(self, per_block, more=0):
                fixed = per_block * self.b + more
                return fixed if self.rnd is None else self.rnd * (WINDOW * per_block) + fixed

            def windows(self, per_window, more=0):
                fixed = per_window * (self.b // WINDOW) + more
                return fixed if self.rnd is None else self.rnd * per_window + fixed

            def first(self):
                return self.rnd is None and self.b == 0

            def has(self, back=0):
                return self.rnd is not None or 0 <= self.b - back < NBLK

        def iterations(eng, one):
            for b in range(LEAD):
                one(Iteration(b))
            with eng.Fori(0, ROUNDS) as rnd:
                for j in range(WINDOW):
                    one(Iteration(LEAD + j, rnd))
            for b in range(LEAD + ROUNDS * WINDOW, NBLK + 1):
                one(Iteration(b))

        def bank0(it):
            return 2 * it.par

        def bank1(it):
            return 2 - 2 * it.par

        @block.sync
        def _(sp):
            def load_x(b, par, split):
                wait(sp, x_lo_done, split)
                src = edges_d[b] if isinstance(b, int) else edges_d[bass.ds(b, 1)].rearrange("a p n -> p (a n)")
                sp.dma_start(x_raw[:, par].rearrange("p k e -> p (k e)"), src).then_inc(x_loaded[par], 16)

            sp.dma_start(w_raw[:, 0:KE * H], w0_d).then_inc(w_loaded, 16)
            load_x(0, 0, 0)
            sp.dma_start(w_raw[:, KE * H:(KE + KH) * H], w1_d).then_inc(w_loaded, 16)
            sp.dma_start(w_raw[:, (KE + KH) * H:], w2_d).then_inc(w_loaded, 16)
            load_x(1, 1, 0)
            with sp.Fori(0, (NBLK - 2) // 2) as g:
                for par in range(2):
                    load_x(g * 2 + (2 + par), par, g * 4 + (2 + 2 * par))
            sp.wait_ge(tile_summed, E // P)
            sp.wait_ge(count_step, 1 + 8 * (NBLK // WINDOW))
            sp.dma_start(rows[:], rows_d.to_broadcast([P, NROWS])).then_inc(late_loaded, 16)
            for dst, src in ((d2_w, d2_d), (wqk, wqk_d), (wv, wv_d), (wo, wo_d), (f1_w, f1_d), (f2_w, f2_d),
                             (w_ih, wih_d), (w_hh, whh_d)):
                sp.dma_start(dst[:].rearrange("p a b -> p (a b)"), src).then_inc(late_loaded, 16)
            for c in range(NC):
                sp.wait_ge(out_ready, c + 1)
                sp.dma_start(out_d[c], hat[:, c]).then_inc(out_stored, 16)
            sp.wait_ge(out_stored, 16 * NC)

        LATE = 16 * 9

        @block.gpsimd
        def _(pool):
            pool.iota(iota_i[:], [[1, N]], base=0, channel_multiplier=0).then_inc(iota_ready, 1)
            pool.memset(ident[:], 0.0).then_inc(ident_zero, 1)
            pool.wait_ge(ident_zero, 1)
            pool.affine_select(out=ident[:], in_=ident[:], compare_op=ALU.not_equal, fill=1.0, base=0,
                               pattern=[[-1, P]], channel_multiplier=1).then_inc(ident_ready, 1)

        @block.scalar
        def _(act):
            act.dma_start(src_i[:], src_d).then_inc(idx_loaded, 16)
            act.dma_start(dst_i[:], dst_d).then_inc(idx_loaded, 16)
            act.dma_start(cols[:], cols_d).then_inc(cols_loaded, 16)
            act.dma_start(m2b[:].rearrange("p a f -> p (a f)"), m2b_d.to_broadcast([P, 2 * H])).then_inc(m2b_loaded, 16)
            act.dma_start(x_rows[:].rearrange("p c f -> p (c f)"), x_rows_d).then_inc(early_loaded, 16)
            act.dma_start(d0_w[:].rearrange("p a b -> p (a b)"), d0_d).then_inc(early_loaded, 16)
            act.dma_start(d1_w[:].rearrange("p a b -> p (a b)"), d1_d).then_inc(early_loaded, 16)
            act.wait_ge(cols_loaded, 16)

            def edge(it):
                if it.has(1):
                    for h in range(2):
                        act.wait_ge(m2_biased, it.count(2, h - 1))
                        wait(act, lo2_done, it.count(2, h - 3))
                        nc.scalar.activation(m2[:, h], m2_in[:, h], ACT.Gelu)
                        wait(act, tile_summed, it.count(4, 2 * h - 6))
                        nc.scalar.activation(m2_hi[:, h], m2_in[:, h], ACT.Gelu).then_inc(gelu2, 1)
                if it.has():
                    for done, lo_done, read, out, out_hi, bank, bias, signal in (
                            (l0_done, lo0_done, l1_done, m0, m0_hi, bank0(it), "m0_b", gelu0),
                            (l1_done, lo1_done, l2_done, m1, m1_hi, bank1(it), "m1_b", gelu1)):
                        for m in range(KH):
                            act.wait_ge(done, it.count(2, m + 1))
                            wait(act, lo_done, it.count(2, m - 1))
                            nc.scalar.activation(out[:, m], ps[:, bank + m], ACT.Gelu, bias=col(bias, m))
                            wait(act, read, it.count(2, 0))
                            nc.scalar.activation(out_hi[:, m], ps[:, bank + m], ACT.Gelu,
                                                 bias=col(bias, m)).then_inc(signal, 1)
                if it.phase == 0 and it.has(1):
                    act.wait_ge(tile_summed, it.count(4, 0))
                    act.wait_ge(count_step, it.windows(8, -7))
                    for r in range(2):
                        nc.scalar.activation(packed[:, r], ps[:, CNT + r], ACT.Copy).then_inc(count_out, 1)

            iterations(act, edge)

            for m in range(KH):
                nc.scalar.activation(sum_T[:, m], ps[:, SUM + m], ACT.Copy, scale=1.0 / 30.0).then_inc(sum_scaled, 1)

            turned = [0]

            def affine(scale=None, bias=None):
                turned[0] += 1
                act.wait_ge(hat_turned, turned[0])
                for k in range(KH):
                    if scale:
                        nc.scalar.activation(act_T[:, k], ps[:, 2 + k], ACT.Identity, bias=col(bias, k),
                                             scale=col(scale, k)).then_inc(act_ready, 1)
                    else:
                        nc.scalar.activation(act_T[:, k], ps[:, 2 + k], ACT.Copy).then_inc(act_ready, 1)

            affine("ln1_g", "ln1_b")
            for m in range(KD):
                act.wait_ge(d0_done, m + 1)
                nc.scalar.activation(d0_T[:, m], ps[:, 4 + m % 4], ACT.Gelu, bias=col("d0_b", m)).then_inc(d0_gelu, 1)
            for m in range(KD):
                act.wait_ge(d1_done, m + 1)
                nc.scalar.activation(d1_T[:, m], ps[:, m % 4], ACT.Gelu, bias=col("d1_b", m)).then_inc(d1_gelu, 1)
            affine()
            for c in range(NC):
                act.wait_ge(qkv_done, c + 1)
                nc.scalar.activation(qk_rows[:, c], ps[:, c % 2], ACT.Copy).then_inc(qkv_out, 1)
                nc.scalar.activation(v_rows[:, c], ps[:, 4 + c % 2, 0:H], ACT.Copy).then_inc(qkv_out, 1)
            act.wait_ge(scores_ready, 1)
            nc.scalar.activation(probs[:], probs[:], ACT.Exp, scale=float(DH) ** -0.5).then_inc(exp_done, 1)
            affine()
            affine("t_ln1_w", "t_ln1_b")
            for m in range(4):
                act.wait_ge(f1_done, m + 1)
                nc.scalar.activation(f1_T[:, m], ps[:, 4 + m], ACT.Relu, bias=col("f1_b", m)).then_inc(f1_relu, 1)
            affine("t_ln2_w", "t_ln2_b")
            for c in range(NC):
                act.wait_ge(rz_ready, c + 1)
                nc.scalar.activation(rz[:, c], rz[:, c], ACT.Sigmoid).then_inc(rz_sig, 1)
                if c:
                    act.wait_ge(cand_ready, c)
                    nc.scalar.activation(cand[:, c - 1], cand[:, c - 1], ACT.Tanh).then_inc(cand_tanh, 1)
            act.wait_ge(cand_ready, NC)
            nc.scalar.activation(cand[:, NC - 1], cand[:, NC - 1], ACT.Tanh).then_inc(cand_tanh, 1)

        @block.vector
        def _(dve):
            W0, W1, W2 = (0, KE * H), (KE * H, (KE + KH) * H), ((KE + KH) * H, (KE + 2 * KH) * H)

            def split_x(par, count_hi, landed, freed):
                dve.wait_ge(x_loaded[par], landed)
                wait(dve, l0_done, freed)
                nc.vector.tensor_copy(x_hi[:, par], x_raw[:, par]).then_inc(x_hi_done, 1)

            def rest_x(par, half, hi):
                dve.wait_ge(x_hi_done, hi)
                ks = slice(2 * half, 2 * half + 2)
                nc.vector.tensor_tensor(x_lo[:, par, ks], x_raw[:, par, ks], x_hi[:, par, ks].bitcast(F32),
                                        ALU.subtract).then_inc(x_lo_done, 1)

            nc.vector.memset(count[:], 0.0).then_inc(count_step, 1)
            for n, (lo, hi) in enumerate((W0, W1, W2)):
                dve.wait_ge(w_loaded, 48)
                nc.vector.tensor_copy(w_hi[:, lo:hi], w_raw[:, lo:hi]).then_inc(w_hi_done, 1)
                if n == 0:
                    split_x(0, 1, 16, 0)
                dve.wait_ge(w_hi_done, n + 1)
                nc.vector.tensor_tensor(w_lo[:, lo:hi], w_raw[:, lo:hi], w_hi[:, lo:hi].bitcast(F32),
                                        ALU.subtract).then_inc(w_split, 1)
                if n == 0:
                    rest_x(0, 0, 1)
                    rest_x(0, 1, 1)
            dve.wait_ge(idx_loaded, 32)
            dve.wait_ge(iota_ready, 1)
            nc.vector.tensor_copy(iota[:], iota_i[:]).then_inc(idx_step, 1)
            nc.vector.tensor_copy(dst_f[:], dst_i[:]).then_inc(idx_step, 1)
            nc.vector.tensor_copy(src_f[:], src_i[:]).then_inc(idx_step, 1)
            dve.wait_ge(idx_step, 3)
            nc.vector.tensor_scalar(src_far[:], src_f[:], float(N // 2), None, ALU.is_ge).then_inc(idx_step, 1)
            dve.wait_ge(idx_step, 4)
            nc.vector.scalar_tensor_tensor(src_in[:], src_far[:], -float(N // 2), src_f[:], ALU.mult,
                                           ALU.add).then_inc(idx_step, 1)
            nc.vector.tensor_scalar(src_unit[:], src_far[:], float((1 << PACK_BITS) - 1), 1.0, ALU.mult,
                                    ALU.add).then_inc(idx_step, 1)
            dve.wait_ge(idx_step, 6)
            dve.wait_ge(m2b_loaded, 16)

            def hot(it, t):
                wait(dve, tile_summed, it.count(4, t - 7))
                at = bass.ds(it.count(4, t), 1)
                nc.vector.tensor_scalar(dst_hot[:, it.par, t], iota[:], dst_f[:, at], None, ALU.is_equal)
                nc.vector.tensor_scalar(pack_hot[:, it.par, t], iota[:, 0:2 * P], src_in[:, at], src_unit[:, at],
                                        ALU.is_equal, ALU.mult)
                nc.vector.tensor_scalar(src_hot[:, it.par, t], iota[:], src_f[:, at], None,
                                        ALU.is_equal).then_inc(hot_ready, 1)

            def rest(it, m, gelu, x, hi, lo, signal, back=0):
                dve.wait_ge(gelu, it.count(2, m + 1 - 2 * back))
                nc.vector.tensor_tensor(lo[:, m], x[:, m], hi[:, m].bitcast(F32), ALU.subtract).then_inc(signal, 1)

            def unpack(it, r):
                dve.wait_ge(count_out, it.windows(2, r - 1))
                dve.wait_ge(count_step, it.windows(8, 4 * r - 7))
                nc.vector.tensor_scalar(part[:, 0], packed[:, r], (1 << PACK_BITS) - 1, None,
                                        ALU.bitwise_and).then_inc(count_step, 1)
                nc.vector.tensor_scalar(part[:, 1], packed[:, r], PACK_BITS, None,
                                        ALU.logical_shift_right).then_inc(count_step, 1)
                for q in range(2):
                    dve.wait_ge(count_step, it.windows(8, 4 * r + q - 6))
                    s = 2 * q + r
                    nc.vector.tensor_tensor(count[:, s], count[:, s], part[:, q], ALU.add).then_inc(count_step, 1)

            def edge(it):
                nxt = 1 - it.par
                more = it.rnd is not None or it.b + 1 < NBLK
                counted = it.phase == 1 and (it.rnd is not None or it.b >= WINDOW)
                if it.has(1):
                    for h in range(2):
                        dve.wait_ge(l2_done, it.count(2, h - 1))
                        wait(dve, gelu2, it.count(2, h - 3))
                        nc.vector.tensor_tensor(m2_in[:, h], ps[:, (2 - bank0(it)) + h], m2b[:].rearrange("p a f -> p (a f)"),
                                                ALU.add).then_inc(m2_biased, 1)
                if more:
                    landed = 16 * ((it.b + 1) // 2 + 1)
                    if it.rnd is not None:
                        landed = it.rnd * (16 * WINDOW // 2) + landed
                    split_x(nxt, None, landed, it.count(2, 0))
                if it.has(1):
                    rest(it, 0, gelu2, m2, m2_hi, m2_lo, lo2_done, 1)
                if more:
                    rest_x(nxt, 0, it.count(1, 2))
                if it.has(1):
                    rest(it, 1, gelu2, m2, m2_hi, m2_lo, lo2_done, 1)
                if counted:
                    unpack(it, 0)
                if it.has():
                    rest(it, 0, gelu0, m0, m0_hi, m0_lo, lo0_done)
                    if more:
                        rest_x(nxt, 1, it.count(1, 2))
                    hot(it, 0)
                    rest(it, 1, gelu0, m0, m0_hi, m0_lo, lo0_done)
                    hot(it, 1)
                    hot(it, 2)
                    rest(it, 0, gelu1, m1, m1_hi, m1_lo, lo1_done)
                    hot(it, 3)
                    rest(it, 1, gelu1, m1, m1_hi, m1_lo, lo1_done)
                if counted:
                    unpack(it, 1)

            iterations(dve, edge)
            for r in range(2):
                unpack(Iteration(NBLK), r)

            steps = [0]

            def link(ins):
                steps[0] += 1
                ins.then_inc(dve_step, 1)
                dve.wait_ge(dve_step, steps[0])

            def norm_stats(src, chunks=range(NC)):
                cs = slice(chunks[0], chunks[-1] + 1)
                for c in chunks:
                    ins = nc.vector.bn_stats(stats[:, c], src[:, c])
                link(ins)
                for c in chunks:
                    ins = nc.vector.bn_aggr(mean_var[:, c], stats[:, c])
                link(ins)
                link(nc.vector.tensor_scalar(var[:, cs], mean_var[:, cs, 1], LN_EPS, None, ALU.add))
                nc.vector.tensor_scalar(half_var[:, cs], var[:, cs], 0.5, None, ALU.mult)
                link(nc.vector.tensor_scalar(sq[:, cs].bitcast(I32), var[:, cs].bitcast(I32), 1, None,
                                             ALU.logical_shift_right))
                link(nc.vector.tensor_scalar(rstd[:, cs].bitcast(I32), sq[:, cs].bitcast(I32), -1.0, float(RSQRT_SEED),
                                             ALU.mult, ALU.add))
                for _ in range(3):
                    link(nc.vector.tensor_tensor(sq[:, cs], rstd[:, cs], rstd[:, cs], ALU.mult))
                    link(nc.vector.tensor_tensor(sq[:, cs], sq[:, cs], half_var[:, cs], ALU.mult))
                    link(nc.vector.scalar_tensor_tensor(rstd[:, cs], sq[:, cs], 1.5, rstd[:, cs], ALU.subtract, ALU.mult,
                                                        reverse0=True))

            def normed(src, out, c):
                return nc.vector.tensor_scalar(out[:, c], src[:, c], mean_var[:, c, 0:1], rstd[:, c:c + 1],
                                               ALU.subtract, ALU.mult)

            def norm(src):
                norm_stats(src)
                for c in range(NC):
                    normed(src, hat, c).then_inc(hat_ready, 1)

            def rows_after(weight, bias, add):
                dve.wait_ge(hat_ready, hats[0])
                link(nc.vector.tensor_tensor(h_rows[:], hat[:], row_all(weight), ALU.mult))
                link(nc.vector.tensor_tensor(h_rows[:], h_rows[:], row_all(bias), ALU.add))
                if add:
                    link(nc.vector.tensor_tensor(skip[:], h_rows[:], row_all(add), ALU.add))

            hats = [0]
            dve.wait_ge(early_loaded, 48)
            dve.wait_ge(sum_turned, 1)
            link(nc.vector.tensor_tensor(res[:], x_rows[:], rows2(0), ALU.add))
            norm(res)
            hats[0] += NC
            dve.wait_ge(late_loaded, LATE)
            rows_after("ln1_g", "ln1_b", "d2_b")
            link(nc.vector.tensor_tensor(skip2[:], x_rows[:], row_all("ln2_b"), ALU.add))
            nc.vector.tensor_tensor(w_rz[:], w_ih[:, :, 0:2 * H], w_hh[:, :, 0:2 * H], ALU.add)
            link(nc.vector.tensor_tensor(b_rz[:], row("b_ih", 0, 2 * H), row("b_hh", 0, 2 * H), ALU.add))
            dve.wait_ge(d2_done, 1)
            link(nc.vector.tensor_tensor(res[:], rows2(4), skip[:], ALU.add))
            norm_stats(res)
            for c in range(NC):
                ins = normed(res, hat, c)
            link(ins)
            link(nc.vector.tensor_tensor(hat[:], hat[:], row_all("ln2_g"), ALU.mult))
            link(nc.vector.tensor_tensor(res[:], hat[:], skip2[:], ALU.add))
            norm_stats(res)
            for c in range(NC):
                normed(res, xp, c).then_inc(hat_ready, 1)
            hats[0] += NC
            dve.wait_ge(hat_ready, hats[0])
            link(nc.vector.tensor_tensor(skip[:], xp[:], row_all("O_b"), ALU.add))
            pairs = [P, HEADS, HEADS, DH]
            for c in range(NC):
                dve.wait_ge(qkv_out, 2 * c + 2)
                q = qk_rows[:, c, 0:H].rearrange("p (h a d) -> p h a d", h=HEADS, a=1).to_broadcast(pairs)
                k = qk_rows[:, c, H:2 * H].rearrange("p (a g d) -> p a g d", a=1, g=HEADS).to_broadcast(pairs)
                view = prod[:, c % 2].rearrange("p (h g d) -> p h g d", h=HEADS, g=HEADS)
                link(nc.vector.tensor_tensor(view, q, k, ALU.mult))
                nc.vector.tensor_reduce(probs[:, c], view, AX_X, ALU.add).then_inc(dve_step, 1)
                steps[0] += 1
            dve.wait_ge(dve_step, steps[0])
            flat = probs[:].rearrange("p c h g -> p (c h) g")

            def each_g(t):
                return t[:].rearrange("p (r a) -> p r a", a=1).to_broadcast([P, NC * HEADS, HEADS])

            link(nc.vector.tensor_reduce(top[:], flat, AX_X, ALU.max))
            nc.vector.tensor_tensor(flat, flat, each_g(top), ALU.subtract).then_inc(scores_ready, 1)
            dve.wait_ge(exp_done, 1)
            link(nc.vector.tensor_reduce(total[:], flat, AX_X, ALU.add))
            link(nc.vector.reciprocal(total[:], total[:]))
            link(nc.vector.tensor_tensor(flat, flat, each_g(total), ALU.mult))
            for c in range(NC):
                sm = probs[:, c].rearrange("p h (a g) -> p h a g", a=1).to_broadcast([P, HEADS, DH, HEADS])
                v = v_rows[:, c].rearrange("p (a g d) -> p a d g", a=1, g=HEADS).to_broadcast([P, HEADS, DH, HEADS])
                view = prod[:, c % 2].rearrange("p (h d g) -> p h d g", h=HEADS, d=DH)
                link(nc.vector.tensor_tensor(view, sm, v, ALU.mult))
                nc.vector.tensor_reduce(x1[:, c].rearrange("p (h d) -> p h d", h=HEADS), view, AX_X,
                                        ALU.add).then_inc(x1_ready, 1)
            dve.wait_ge(gathered, 1)
            dve.wait_ge(x1_ready, NC)
            for c in range(NC):
                nc.vector.tensor_tensor(hat[:, c], x1[:, c], rows2(0)[:, c], ALU.mult).then_inc(hat_ready, 1)
            hats[0] += NC
            dve.wait_ge(o_done, 1)
            link(nc.vector.tensor_tensor(res[:], rows2(4), skip[:], ALU.add))
            norm(res)
            hats[0] += NC
            rows_after("t_ln1_w", "t_ln1_b", "f2_b")
            dve.wait_ge(f2_done, 1)
            link(nc.vector.tensor_tensor(res[:], rows2(0), skip[:], ALU.add))
            norm(res)
            hats[0] += NC
            rows_after("t_ln2_w", "t_ln2_b", None)
            for c in range(NC):
                dve.wait_ge(gru_done, c + 1)
                nc.vector.tensor_tensor(rz[:, c], ps[:, 2 * (c % 2)], b_rz[:], ALU.add).then_inc(rz_ready, 1)
                nc.vector.tensor_tensor(gn[:, c, 0:H], ps[:, 2 * (c % 2) + 1, 0:H], row("b_ih", 2 * H, H), ALU.add)
                link(nc.vector.tensor_tensor(gn[:, c, H:2 * H], ps[:, 2 * (c % 2) + 1, H:2 * H], row("b_hh", 2 * H, H),
                                             ALU.add))
                dve.wait_ge(rz_sig, c + 1)
                link(nc.vector.tensor_tensor(gn[:, c, H:2 * H], gn[:, c, H:2 * H], rz[:, c, 0:H], ALU.mult))
                nc.vector.tensor_tensor(cand[:, c], gn[:, c, 0:H], gn[:, c, H:2 * H], ALU.add).then_inc(cand_ready, 1)
            for c in range(NC):
                dve.wait_ge(cand_tanh, c + 1)
                link(nc.vector.tensor_tensor(res[:, c], h_rows[:, c], cand[:, c], ALU.subtract))
                link(nc.vector.tensor_tensor(res[:, c], res[:, c], rz[:, c, H:2 * H], ALU.mult))
                link(nc.vector.tensor_tensor(res[:, c], res[:, c], cand[:, c], ALU.add))
                link(nc.vector.tensor_tensor(res[:, c], res[:, c], xp[:, c], ALU.add))
            norm_stats(res)
            for c in range(NC):
                normed(res, hat, c).then_inc(out_ready, 1)

        @block.tensor
        def _(pe):
            def w(n, k, m, part):
                at = ((0, KE, KE + KH)[n] + k) * H
                return part[:, at + m * P:at + (m + 1) * P]

            def passes(a_hi, a_lo, b_hi, b_lo):
                return (a_hi, b_hi), (a_hi, b_lo), (a_lo, b_hi)

            def layer(it, n, bank, hi, lo, chunks, free, free_count, in_ready, in_count, done):
                for m in range(KH):
                    wait(pe, free, it.count(*free_count(m)))
                    for k in range(chunks):
                        if m == 0:
                            for s, value in in_ready(k):
                                pe.wait_ge(s, value)
                        ops = passes(w(n, k, m, w_hi), w(n, k, m, w_lo), hi[:, k], lo[:, k])
                        for i, (a, b) in enumerate(ops):
                            last = nc.tensor.matmul(ps[:, bank + m], a, b, start=(k == 0 and i == 0),
                                                    stop=(k == chunks - 1 and i == 2))
                    last.then_inc(done, 1)

            def sum_tile(it, t):
                par = 1 - it.par
                pe.wait_ge(hot_ready, it.count(4, t - 3))
                pe.wait_ge(lo2_done, it.count(2, t // 2 - 1))
                lone = it.rnd is None
                first, final = lone and it.b == 1 and t == 0, lone and it.b == NBLK and t == TB - 1
                phase = (it.phase - 1) % WINDOW
                if phase == 0 and t == 0 and not first:
                    pe.wait_ge(count_out, it.windows(2, 0))
                half, at = t // 2, (t % 2) * H
                for m in range(KH):
                    for i, part in enumerate((m2_hi, m2_lo)):
                        nc.tensor.matmul(ps[:, SUM + m], part[:, half, at + m * P:at + (m + 1) * P], src_hot[:, par, t],
                                         start=(first and i == 0), stop=(final and i == 1), skip_group_check=True)
                for r in range(2):
                    last = nc.tensor.matmul(ps[:, CNT + r], pack_hot[:, par, t, r * P:(r + 1) * P], dst_hot[:, par, t],
                                            start=(phase == 0 and t == 0), stop=(phase == WINDOW - 1 and t == TB - 1),
                                            skip_group_check=True)
                last.then_inc(tile_summed, 1)

            def messages(it):
                for t in range(TB):
                    h = t // 2
                    if t % 2 == 0:
                        pe.wait_ge(gelu0, it.count(2, h + 1))
                    if t == 0:
                        pe.wait_ge(lo1_done, it.count(2, 2))
                    out = ps[:, bank0(it) + h, (t % 2) * H:(t % 2 + 1) * H]
                    for k in range(KH):
                        e = slice(t * P, (t + 1) * P)
                        at = (KE + KH + k) * H
                        ops = passes(m1_hi[:, k, e], m1_lo[:, k, e], w_hi[:, at:at + H], w_lo[:, at:at + H])
                        for i, (a, b) in enumerate(ops):
                            last = nc.tensor.matmul(out, a, b, start=(k == 0 and i == 0), stop=(k == KH - 1 and i == 2))
                    if t % 2:
                        last.then_inc(l2_done, 1)

            def edge(it):
                if it.has():
                    if it.first():
                        pe.wait_ge(w_split, 1)
                    layer(it, 0, bank0(it), x_hi[:, it.par], x_lo[:, it.par], KE, gelu1, lambda m: (2, m - 1),
                          lambda k: [(x_lo_done, it.count(2, k // 2 + 1))] if k % 2 == 0 else [], None, l0_done)
                if it.has(1):
                    sum_tile(it, 0)
                    sum_tile(it, 1)
                if it.has():
                    if it.first():
                        pe.wait_ge(w_split, 3)
                    layer(it, 1, bank1(it), m0_hi, m0_lo, KH, m2_biased, lambda m: (2, m - 1),
                          lambda k: [(lo0_done, it.count(2, k + 1))], None, l1_done)
                if it.has(1):
                    sum_tile(it, 2)
                    sum_tile(it, 3)
                if it.has():
                    messages(it)

            iterations(pe, edge)

            def turn(src, k, c, out):
                return nc.tensor.transpose(out, src, ident[:])

            pe.wait_ge(sum_scaled, 2)
            pe.wait_ge(ident_ready, 1)
            for c in range(NC):
                for m in range(KH):
                    last = nc.tensor.transpose(rows2(0)[:, c, m * P:(m + 1) * P], sum_T[:, m, c * P:(c + 1) * P], ident[:])
            last.then_inc(sum_turned, 1)
            hats = [0]
            acts = [0]

            def turn_rows(src):
                for c in range(NC):
                    hats[0] += 1
                    pe.wait_ge(hat_ready, hats[0])
                    for k in range(KH):
                        last = nc.tensor.transpose(ps[:, 2 + k, c * P:(c + 1) * P], src[:, c, k * P:(k + 1) * P], ident[:])
                last.then_inc(hat_turned, 1)
                acts[0] += KH
                pe.wait_ge(act_ready, acts[0])

            def to_columns(weights, chunks, m, rhs, bank):
                for k in range(chunks):
                    last = nc.tensor.matmul(ps[:, bank], weights[:, k, m * P:(m + 1) * P], rhs[:, k], start=(k == 0),
                                            stop=(k == chunks - 1))
                return last

            def to_rows(lhs, chunks, weights, bank):
                for c in range(NC):
                    for k in range(chunks):
                        last = nc.tensor.matmul(rows2(bank)[:, c], lhs[:, k, c * P:(c + 1) * P], weights[:, k],
                                                start=(k == 0), stop=(k == chunks - 1))
                return last

            turn_rows(hat)
            pe.wait_ge(early_loaded, 48)
            for m in range(KD):
                if m >= 4:
                    pe.wait_ge(d0_gelu, m - 3)
                to_columns(d0_w, KH, m, act_T, 4 + m % 4).then_inc(d0_done, 1)
            pe.wait_ge(d0_gelu, KD)
            for m in range(KD):
                if m >= 4:
                    pe.wait_ge(d1_gelu, m - 3)
                to_columns(d1_w, KD, m, d0_T, m % 4).then_inc(d1_done, 1)
            pe.wait_ge(d1_gelu, KD)
            pe.wait_ge(late_loaded, LATE)
            to_rows(d1_T, KD, d2_w, 4).then_inc(d2_done, 1)
            turn_rows(xp)
            for c in range(NC):
                if c >= 2:
                    pe.wait_ge(qkv_out, 2 * c - 2)
                for bank, weights, width in ((c % 2, wqk, 2 * H), (4 + c % 2, wv, H)):
                    for k in range(KH):
                        last = nc.tensor.matmul(ps[:, bank, 0:width], act_T[:, k, c * P:(c + 1) * P], weights[:, k],
                                                start=(k == 0), stop=(k == KH - 1))
                last.then_inc(qkv_done, 1)
            pe.wait_ge(count_step, 1 + 8 * (NBLK // WINDOW))
            pe.wait_ge(x1_ready, NC)
            to_rows(count, NC, x1, 0).then_inc(gathered, 1)
            turn_rows(hat)
            to_rows(act_T, KH, wo, 4).then_inc(o_done, 1)
            turn_rows(hat)
            for m in range(4):
                to_columns(f1_w, KH, m, act_T, 4 + m).then_inc(f1_done, 1)
            pe.wait_ge(f1_relu, 4)
            to_rows(f1_T, 4, f2_w, 0).then_inc(f2_done, 1)
            turn_rows(hat)
            for c in range(NC):
                if c >= 2:
                    pe.wait_ge(cand_ready, c - 1)
                bank = 2 * (c % 2)
                for k in range(KH):
                    nc.tensor.matmul(ps[:, bank], act_T[:, k, c * P:(c + 1) * P], w_rz[:, k], start=(k == 0),
                                     stop=(k == KH - 1))
                for at, wn in ((0, w_ih), (H, w_hh)):
                    for k in range(KH):
                        last = nc.tensor.matmul(ps[:, bank + 1, at:at + H], act_T[:, k, c * P:(c + 1) * P],
                                                wn[:, k, 2 * H:3 * H], start=(k == 0), stop=(k == KH - 1))
                last.then_inc(gru_done, 1)


def kernel(**inputs):
    import numpy as np
    import concourse.bacc as bacc
    from concourse.bass_utils import run_bass_kernel_spmd

    a = {k: np.asarray(v) for k, v in inputs.items()}

    def chunked(w):
        return np.ascontiguousarray(w.reshape(-1, P, w.shape[1]).transpose(1, 0, 2).reshape(P, -1))

    L0, L1 = "L0_gnn_", "L1_gnn_"
    col_src = {"m0_b": L0 + "m0_b", "m1_b": L0 + "m1_b", "ln1_g": L0 + "ln1_g", "ln1_b": L0 + "ln1_b",
               "d0_b": L0 + "d0_b", "d1_b": L0 + "d1_b", "t_ln1_w": L1 + "ln1_w", "t_ln1_b": L1 + "ln1_b",
               "f1_b": L1 + "f1_b", "t_ln2_w": L1 + "ln2_w", "t_ln2_b": L1 + "ln2_b"}
    row_src = {"ln1_g": L0 + "ln1_g", "ln1_b": L0 + "ln1_b", "d2_b": L0 + "d2_b", "ln2_g": L0 + "ln2_g",
               "ln2_b": L0 + "ln2_b", "O_b": L1 + "O_b", "t_ln1_w": L1 + "ln1_w", "t_ln1_b": L1 + "ln1_b",
               "f2_b": L1 + "f2_b", "t_ln2_w": L1 + "ln2_w", "t_ln2_b": L1 + "ln2_b", "b_ih": L1 + "gru_b_ih",
               "b_hh": L1 + "gru_b_hh"}
    data = [
        ("x_rows", chunked(a["x"])),
        ("edges", np.ascontiguousarray(a["edge_attr_512"].reshape(NBLK, BLK, KE, P).transpose(0, 3, 2, 1)
                                       .reshape(NBLK, P, KE * BLK))),
        ("src", np.ascontiguousarray(a["src"].reshape(E // P, P).T)),
        ("dst", np.ascontiguousarray(a["dst"].reshape(E // P, P).T)),
        ("w0", chunked(a[L0 + "m0_w"])), ("w1", chunked(a[L0 + "m1_w"])), ("w2", chunked(a[L0 + "m2_w"])),
        ("m2b", np.concatenate([a[L0 + "m2_b"]] * 2).reshape(1, 2 * H)),
        ("cols", np.ascontiguousarray(np.concatenate([a[col_src[n]].reshape(-1, P) for n in COLS]).T)),
        ("rows", np.concatenate([a[row_src[n]] for n in ROWS]).reshape(1, NROWS)),
        ("d0", chunked(a[L0 + "d0_w"])), ("d1", chunked(a[L0 + "d1_w"])), ("d2", chunked(a[L0 + "d2_w"])),
        ("wqk", chunked(np.concatenate([a[L1 + "Wq"], a[L1 + "Wk"]], axis=1))), ("wv", chunked(a[L1 + "Wv"])),
        ("wo", chunked(a[L1 + "O_w"])), ("f1", chunked(a[L1 + "f1_w"])), ("f2", chunked(a[L1 + "f2_w"])),
        ("wih", chunked(a[L1 + "gru_w_ih"])), ("whh", chunked(a[L1 + "gru_w_hh"])),
    ]
    nc = bacc.Bacc("TRN2", target_bir_lowering=False, num_devices=1)
    aps = [nc.dram_tensor(f"in_{n}_dram", v.shape, mybir.dt.from_np(v.dtype), kind="ExternalInput").ap() for n, v in data]
    out = nc.dram_tensor("out_dram", (NC, P, H), F32, kind="ExternalOutput").ap()
    gnn_kernel(nc, *aps, out)
    result = run_bass_kernel_spmd(nc, [{f"in_{n}_dram": v for n, v in data}], core_ids=[0])
    return result.results[0]["out_dram"].reshape(N, H)
```

```python
from contextlib import ExitStack

import concourse.bass as bass
from concourse import mybir

F32 = mybir.dt.float32
F32R = mybir.dt.float32r
BF16 = mybir.dt.bfloat16
FP16 = mybir.dt.float16
I32 = mybir.dt.int32
ALU = mybir.AluOpType
ACT = mybir.ActivationFunctionType
AX_X = mybir.AxisListType.X

P = 128
N = 512
H = 256
E = 16384
EIN = 512
D = 1024
HEADS = 8
DH = H // HEADS
BLK = 512
TB = BLK // P
NBLK = E // BLK
KE = EIN // P
KH = H // P
KD = D // P
NC = N // P
LN_EPS = 1e-5
WINDOW = 4
PACK_BITS = 12
RSQRT_SEED = 0x5F3759DF - (1 << 22)

COLS = {}
_at = 0
for _name, _n in (("m0_b", KH), ("m1_b", KH), ("ln1_g", KH), ("ln1_b", KH), ("d0_b", KD), ("d1_b", KD),
                  ("t_ln1_w", KH), ("t_ln1_b", KH), ("f1_b", 4), ("t_ln2_w", KH), ("t_ln2_b", KH)):
    COLS[_name] = (_at, _n)
    _at += _n
NCOLS = _at
ROWS = {}
_at = 0
for _name, _n in (("ln1_g", H), ("ln1_b", H), ("d2_b", H), ("ln2_g", H), ("ln2_b", H), ("O_b", H),
                  ("t_ln1_w", H), ("t_ln1_b", H), ("f2_b", H), ("t_ln2_w", H), ("t_ln2_b", H),
                  ("b_ih", 3 * H), ("b_hh", 3 * H)):
    ROWS[_name] = (_at, _n)
    _at += _n
NROWS = _at


def gnn_kernel(nc, x_rows_d, edges_d, src_d, dst_d, w0_d, w1_d, w2_d, m2b_d, cols_d, rows_d, d0_d, d1_d, d2_d,
               wqk_d, wv_d, wo_d, f1_d, f2_d, wih_d, whh_d, out_d):
    ctx = ExitStack()
    with ctx:
        mem = [ctx]

        def sb(name, shape, dt=F32):
            return mem[0].enter_context(nc.sbuf_tensor(name, shape, dt))

        def sem(name):
            return ctx.enter_context(nc.semaphore(name))

        x_rows = sb("x_rows", [P, NC, H])
        cols = sb("cols", [P, NCOLS])
        d0_w = sb("d0_w", [P, KH, D])
        d1_w = sb("d1_w", [P, KD, D])
        count = sb("count", [P, NC, N])
        ident = sb("ident", [P, P])

        edge_mem = ExitStack()
        mem[0] = edge_mem
        w_raw = sb("w_raw", [P, (KE + 2 * KH) * H])
        w_hi = sb("w_hi", [P, (KE + 2 * KH) * H], F32R)
        w_lo = sb("w_lo", [P, (KE + 2 * KH) * H], F32R)
        m2b = sb("m2b", [P, 2, H])
        x_raw = sb("x_raw", [P, 2, KE, BLK])
        x_hi = sb("x_hi", [P, 2, KE, BLK], F32R)
        x_lo = sb("x_lo", [P, 2, KE, BLK], F32R)
        m0 = sb("m0", [P, KH, BLK])
        m0_hi = sb("m0_hi", [P, KH, BLK], F32R)
        m0_lo = sb("m0_lo", [P, KH, BLK], F32R)
        m1 = sb("m1", [P, KH, BLK])
        m1_hi = sb("m1_hi", [P, KH, BLK], F32R)
        m1_lo = sb("m1_lo", [P, KH, BLK], F32R)
        m2_in = sb("m2_in", [P, 2, 2 * H])
        m2 = sb("m2", [P, 2, 2 * H])
        m2_hi = sb("m2_hi", [P, 2, 2 * H], F32R)
        m2_lo = sb("m2_lo", [P, 2, 2 * H], F32R)
        src_hot = sb("src_hot", [P, 2, TB, N], F32R)
        dst_hot = sb("dst_hot", [P, 2, TB, N], BF16)
        pack_hot = sb("pack_hot", [P, 2, TB, 2 * P], BF16)
        iota_i = sb("iota_i", [P, N], I32)
        iota = sb("iota", [P, N], FP16)
        src_i = sb("src_i", [P, E // P], I32)
        dst_i = sb("dst_i", [P, E // P], I32)
        src_f = sb("src_f", [P, E // P])
        dst_f = sb("dst_f", [P, E // P])
        src_far = sb("src_far", [P, E // P])
        src_in = sb("src_in", [P, E // P])
        src_unit = sb("src_unit", [P, E // P])
        packed = w_raw[:, 0:2 * N].bitcast(I32).rearrange("p (r n) -> p r n", r=2)
        part = w_raw[:, 2 * N:4 * N].bitcast(I32).rearrange("p (r n) -> p r n", r=2)
        edge_mem.close()

        node_mem = ExitStack()
        mem[0] = node_mem
        rows = sb("rows", [P, NROWS])
        res = sb("res", [P, NC, H])
        hat = sb("hat", [P, NC, H])
        stats = sb("stats", [P, NC, 6])
        mean_var = sb("mean_var", [P, NC, 2])
        half_var = sb("half_var", [P, NC])
        rstd = sb("rstd", [P, NC])
        sq = sb("sq", [P, NC])
        h_rows = sb("h_rows", [P, NC, H])
        skip = sb("skip", [P, NC, H])
        skip2 = sb("skip2", [P, NC, H])
        xp = sb("xp", [P, NC, H])
        act_T = sb("act_T", [P, KH, N])
        bias_sum = sb("bias_sum", [P, 2, H])
        node_mlp_mem = ExitStack()
        mem[0] = node_mlp_mem
        d_T = sb("d_T", [P, 4, N])
        d0_hi = sb("d0_hi", [P, KD, N], F32R)
        d0_lo = sb("d0_lo", [P, KD, N], F32R)
        d1_hi = sb("d1_hi", [P, KD, N], F32R)
        d1_lo = sb("d1_lo", [P, KD, N], F32R)
        d1w_hi = sb("d1w_hi", [P, 2, KD, P], F32R)
        d1w_lo = sb("d1w_lo", [P, 2, KD, P], F32R)
        d2w_hi = sb("d2w_hi", [P, KD, H], F32R)
        d2w_lo = sb("d2w_lo", [P, KD, H], F32R)
        sum_T = d_T[:, 0:KH]
        d2_w = d0_w[:].rearrange("p k (j n) -> p (k j) n", n=H)
        node_mlp_mem.close()
        second_mem = ExitStack()
        mem[0] = second_mem
        sb("under_d_T", [P, 4, N])
        wqk = sb("wqk", [P, KH, 2 * H])
        wv = sb("wv", [P, KH, H])
        wo = sb("wo", [P, KH, H])
        f1_w = sb("f1_w", [P, KH, 2 * H])
        f2_w = sb("f2_w", [P, 4, H])
        w_ih = sb("w_ih", [P, KH, 3 * H])
        w_hh = sb("w_hh", [P, KH, 3 * H])
        w_rz = sb("w_rz", [P, KH, 2 * H])
        qk_rows = sb("qk_rows", [P, NC, 2 * H])
        v_rows = sb("v_rows", [P, NC, H])
        prod = sb("prod", [P, 2, HEADS * HEADS * DH])
        probs = sb("probs", [P, NC, HEADS, HEADS])
        top = sb("top", [P, NC * HEADS])
        total = sb("total", [P, NC * HEADS])
        x1 = sb("x1", [P, NC, H])
        b_rz = sb("b_rz", [P, 2 * H])
        b_n = sb("b_n", [P, 2 * H])
        rz = sb("rz", [P, NC, 2 * H])
        gn = sb("gn", [P, NC, 2 * H])
        cand = sb("cand", [P, NC, H])
        f1_T = sb("f1_T", [P, 4, N])
        second_mem.close()
        node_mem.close()
        mem[0] = ctx

        ps = ctx.enter_context(nc.psum_tensor("ps", [P, 8, 512], F32))
        SUM, CNT = 4, 6

        SUMS = (2, 3)
        GRU_BANKS = (0, 4, 6, 0)
        CHUNKS = (range(0, NC // 2), range(NC // 2, NC))
        NH = N // 2
        HALF = (slice(0, NH), slice(NH, N))

        def rows4(bank):
            return ps[:, bank:bank + NC, 0:H]

        def col(name, i):
            at, _ = COLS[name]
            return cols[:, at + i:at + i + 1]

        def row(name, lo=0, n=None):
            at, size = ROWS[name]
            return rows[:, at + lo:at + lo + (n or size)]

        def product_rows(c):
            return ps[:, 4 + c, 0:H]

        def sum_rows(c):
            return ps[:, (0, 1, CNT, CNT + 1)[c], 0:H]

        def turned_bank(half, k):
            return ps[:, 2 + half, k * NH:(k + 1) * NH]

        def row_half(r):
            return r.rearrange("p (a f) -> p a f", a=1).to_broadcast([P, NC // 2, H])

        def bias_row(i):
            return bias_sum[:, i]

        def row_all(name):
            return row(name).rearrange("p (a f) -> p a f", a=1).to_broadcast([P, NC, H])

        x_loaded = [sem("x_loaded0"), sem("x_loaded1")]
        w_loaded, m2b_loaded, idx_loaded = sem("w_loaded"), sem("m2b_loaded"), sem("idx_loaded")
        cols_loaded, early_loaded, rows_loaded = sem("cols_loaded"), sem("early_loaded"), sem("rows_loaded")
        d2_loaded, second_loaded = sem("d2_loaded"), sem("second_loaded")
        iota_ready, iota_cast = sem("iota_ready"), sem("iota_cast")
        ident_zero, ident_ready = sem("ident_zero"), sem("ident_ready")
        w_hi_done, w_split = sem("w_hi_done"), sem("w_split")
        idx_step = sem("idx_step")
        x_hi_done, x_lo_done = sem("x_hi_done"), sem("x_lo_done")
        l0_done, l1_done, l2_done = sem("l0_done"), sem("l1_done"), sem("l2_done")
        gelu0, gelu1, gelu2 = sem("gelu0"), sem("gelu1"), sem("gelu2")
        lo0_done, lo1_done, lo2_done = sem("lo0_done"), sem("lo1_done"), sem("lo2_done")
        m2_biased = sem("m2_biased")
        hot_ready, tile_summed = sem("hot_ready"), sem("tile_summed")
        count_out, count_step = sem("count_out"), sem("count_step")
        sum_scaled, sum_turned = sem("sum_scaled"), sem("sum_turned")
        hat_ready, hat_turned, act_ready = sem("hat_ready"), sem("hat_turned"), sem("act_ready")
        skip_ready = sem("skip_ready")
        d0_done, d1_done, d2_done = sem("d0_done"), sem("d1_done"), sem("d2_done")
        gelu_out, gelu_split = sem("gelu_out"), sem("gelu_split")
        d1w_hi_done, d1w_split = sem("d1w_hi_done"), sem("d1w_split")
        d2w_hi_done, d2w_split = sem("d2w_hi_done"), sem("d2w_split")
        qkv_done, qkv_out = sem("qkv_done"), sem("qkv_out")
        scores_ready, exp_done = sem("scores_ready"), sem("exp_done")
        prod_ready, prod_summed, score_read = sem("prod_ready"), sem("prod_summed"), sem("score_read")
        x1_out, x1_ready, gathered = sem("x1_out"), sem("x1_ready"), sem("gathered")
        rz_weights = sem("rz_weights")
        bias_sums = sem("bias_sums")
        o_done, f1_done, f1_relu, f2_done = sem("o_done"), sem("f1_done"), sem("f1_relu"), sem("f2_done")
        gru_done, rz_ready, rz_sig = sem("gru_done"), sem("rz_ready"), sem("rz_sig")
        gn_ready, cand_ready, cand_tanh = sem("gn_ready"), sem("cand_ready"), sem("cand_tanh")
        out_ready, out_stored = sem("out_ready"), sem("out_stored")
        dve_step = sem("dve_step")

        block = ctx.enter_context(nc.Block())

        def wait(eng, s, value):
            if not isinstance(value, int) or value > 0:
                eng.wait_ge(s, value)

        LEAD = 2
        ROUNDS = (NBLK - LEAD - 2) // WINDOW

        class Iteration:
            def __init__(self, b, rnd=None):
                self.b, self.rnd = b, rnd
                self.phase, self.par = b % WINDOW, b % 2

            def count(self, per_block, more=0):
                fixed = per_block * self.b + more
                return fixed if self.rnd is None else self.rnd * (WINDOW * per_block) + fixed

            def windows(self, per_window, more=0):
                fixed = per_window * (self.b // WINDOW) + more
                return fixed if self.rnd is None else self.rnd * per_window + fixed

            def first(self):
                return self.rnd is None and self.b == 0

            def has(self, back=0):
                return self.rnd is not None or 0 <= self.b - back < NBLK

        def iterations(eng, one):
            for b in range(LEAD):
                one(Iteration(b))
            with eng.Fori(0, ROUNDS) as rnd:
                for j in range(WINDOW):
                    one(Iteration(LEAD + j, rnd))
            for b in range(LEAD + ROUNDS * WINDOW, NBLK + 1):
                one(Iteration(b))

        def bank0(it):
            return 2 * it.par

        def bank1(it):
            return 2 - 2 * it.par

        @block.sync
        def _(sp):
            def load_x(b, par, split):
                wait(sp, x_lo_done, split)
                src = edges_d[b] if isinstance(b, int) else edges_d[bass.ds(b, 1)].rearrange("a p n -> p (a n)")
                sp.dma_start(x_raw[:, par].rearrange("p k e -> p (k e)"), src).then_inc(x_loaded[par], 16)

            sp.dma_start(w_raw[:, 0:KE * H], w0_d).then_inc(w_loaded, 16)
            load_x(0, 0, 0)
            sp.dma_start(w_raw[:, KE * H:(KE + KH) * H], w1_d).then_inc(w_loaded, 16)
            sp.dma_start(w_raw[:, (KE + KH) * H:], w2_d).then_inc(w_loaded, 16)
            load_x(1, 1, 0)
            with sp.Fori(0, (NBLK - 2) // 2) as g:
                for par in range(2):
                    load_x(g * 2 + (2 + par), par, g * 4 + (2 + 2 * par))
            sp.wait_ge(tile_summed, E // P)
            sp.wait_ge(count_step, 1 + 8 * (NBLK // WINDOW))
            sp.dma_start(rows[:], rows_d.to_broadcast([P, NROWS])).then_inc(rows_loaded, 16)
            sp.wait_ge(d0_done, 2 * KD)
            sp.dma_start(d2_w, d2_d.rearrange("p (a b) -> p a b", b=H)).then_inc(d2_loaded, 16)
            sp.wait_ge(d1_done, KD)
            for dst, src in ((wqk, wqk_d), (wv, wv_d), (w_ih, wih_d), (w_hh, whh_d), (wo, wo_d), (f1_w, f1_d), (f2_w, f2_d)):
                sp.dma_start(dst[:].rearrange("p a b -> p (a b)"), src).then_inc(second_loaded, 16)
            for c in range(NC):
                sp.wait_ge(out_ready, c + 1)
                sp.dma_start(out_d[c], hat[:, c]).then_inc(out_stored, 16)
            sp.wait_ge(out_stored, 16 * NC)

        SECOND = 16 * 7

        @block.gpsimd
        def _(pool):
            pool.iota(iota_i[:], [[1, N]], base=0, channel_multiplier=0).then_inc(iota_ready, 1)
            pool.memset(ident[:], 0.0).then_inc(ident_zero, 1)
            pool.wait_ge(ident_zero, 1)
            pool.affine_select(out=ident[:], in_=ident[:], compare_op=ALU.not_equal, fill=1.0, base=0,
                               pattern=[[-1, P]], channel_multiplier=1).then_inc(ident_ready, 1)
            pool.wait_ge(rows_loaded, 16)
            for i, (norm_bias, bias) in enumerate((("ln1_b", "d2_b"), ("t_ln1_b", "f2_b"))):
                pool.tensor_tensor(bias_sum[:, i], row(norm_bias), row(bias), ALU.add).then_inc(bias_sums, 2)
            pool.wait_ge(second_loaded, SECOND)
            pool.tensor_tensor(w_rz[:], w_ih[:, :, 0:2 * H], w_hh[:, :, 0:2 * H], ALU.add).then_inc(rz_weights, 1)
            pool.tensor_tensor(b_rz[:], row("b_ih", 0, 2 * H), row("b_hh", 0, 2 * H), ALU.add).then_inc(bias_sums, 1)
            pool.tensor_copy(b_n[:, 0:H], row("b_ih", 2 * H, H)).then_inc(bias_sums, 1)
            pool.tensor_copy(b_n[:, H:2 * H], row("b_hh", 2 * H, H)).then_inc(bias_sums, 1)

        @block.scalar
        def _(act):
            act.dma_start(src_i[:], src_d).then_inc(idx_loaded, 16)
            act.dma_start(dst_i[:], dst_d).then_inc(idx_loaded, 16)
            act.dma_start(cols[:], cols_d).then_inc(cols_loaded, 16)
            act.dma_start(m2b[:].rearrange("p a f -> p (a f)"), m2b_d.to_broadcast([P, 2 * H])).then_inc(m2b_loaded, 16)
            act.dma_start(x_rows[:].rearrange("p c f -> p (c f)"), x_rows_d).then_inc(early_loaded, 16)
            act.dma_start(d0_w[:].rearrange("p a b -> p (a b)"), d0_d).then_inc(early_loaded, 16)
            act.dma_start(d1_w[:].rearrange("p a b -> p (a b)"), d1_d).then_inc(early_loaded, 16)
            act.wait_ge(cols_loaded, 16)

            def edge(it):
                if it.has(1):
                    for h in range(2):
                        act.wait_ge(m2_biased, it.count(2, h - 1))
                        wait(act, lo2_done, it.count(2, h - 3))
                        nc.scalar.activation(m2[:, h], m2_in[:, h], ACT.Gelu)
                        wait(act, tile_summed, it.count(4, 2 * h - 6))
                        nc.scalar.activation(m2_hi[:, h], m2_in[:, h], ACT.Gelu).then_inc(gelu2, 1)
                if it.has():
                    for done, lo_done, read, out, out_hi, bank, bias, signal in (
                            (l0_done, lo0_done, l1_done, m0, m0_hi, bank0(it), "m0_b", gelu0),
                            (l1_done, lo1_done, l2_done, m1, m1_hi, bank1(it), "m1_b", gelu1)):
                        for m in range(KH):
                            act.wait_ge(done, it.count(2, m + 1))
                            wait(act, lo_done, it.count(2, m - 1))
                            nc.scalar.activation(out[:, m], ps[:, bank + m], ACT.Gelu, bias=col(bias, m))
                            wait(act, read, it.count(2, 0))
                            nc.scalar.activation(out_hi[:, m], ps[:, bank + m], ACT.Gelu,
                                                 bias=col(bias, m)).then_inc(signal, 1)
                if it.phase == 0 and it.has(1):
                    act.wait_ge(tile_summed, it.count(4, 0))
                    act.wait_ge(count_step, it.windows(8, -7))
                    for r in range(2):
                        nc.scalar.activation(packed[:, r], ps[:, CNT + r], ACT.Copy).then_inc(count_out, 1)

            iterations(act, edge)

            turned = [0]

            def affine(half, scale=None, bias=None):
                turned[0] += 1
                act.wait_ge(hat_turned, turned[0])
                for k in range(KH):
                    out, src = act_T[:, k, HALF[half]], turned_bank(half, k)
                    if scale:
                        nc.scalar.activation(out, src, ACT.Identity, bias=col(bias, k),
                                             scale=col(scale, k)).then_inc(act_ready, 1)
                    else:
                        nc.scalar.activation(out, src, ACT.Copy).then_inc(act_ready, 1)

            def round_d1w(m):
                if m >= 2:
                    act.wait_ge(d1_done, m - 1)
                nc.scalar.activation(d1w_hi[:, m % 2], d1_w[:, :, m * P:(m + 1) * P], ACT.Copy).then_inc(d1w_hi_done, 1)

            def gelu_split_out(i, out, bias, hi):
                if i >= 4:
                    act.wait_ge(gelu_split, i - 3)
                nc.scalar.activation(d_T[:, i % 4, 0:hi.shape[-1]], out, ACT.Gelu, bias=bias)
                nc.scalar.activation(hi, out, ACT.Gelu, bias=bias).then_inc(gelu_out, 1)

            act.wait_ge(early_loaded, 48)
            round_d1w(0)
            round_d1w(1)
            affine(0, "ln1_g", "ln1_b")
            for i in range(2 * KD):
                half, m = divmod(i, KD)
                if i == 2:
                    affine(1, "ln1_g", "ln1_b")
                act.wait_ge(d0_done, i + 1)
                gelu_split_out(i, ps[:, 4 + m % 4, 0:NH], col("d0_b", m), d0_hi[:, m, HALF[half]])
            for m in range(KD):
                act.wait_ge(d1_done, m + 1)
                gelu_split_out(2 * KD + m, ps[:, m % 4], col("d1_b", m), d1_hi[:, m])
                if m + 2 < KD:
                    round_d1w(m + 2)
                if m in (3, 4):
                    act.wait_ge(d2_loaded, 16)
                    ks = slice((m - 3) * 4, (m - 3) * 4 + 4)
                    nc.scalar.activation(d2w_hi[:, ks], d2_w[:, ks], ACT.Copy).then_inc(d2w_hi_done, 1)
            for c in range(NC):
                if c % 2 == 0:
                    affine(c // 2)
                act.wait_ge(qkv_done, c + 1)
                nc.scalar.activation(qk_rows[:, c], ps[:, c % 2], ACT.Copy).then_inc(qkv_out, 1)
                nc.scalar.activation(v_rows[:, c], ps[:, 4 + c % 2, 0:H], ACT.Copy).then_inc(qkv_out, 1)
            act.wait_ge(scores_ready, 1)
            nc.scalar.activation(probs[:], probs[:], ACT.Exp, scale=float(DH) ** -0.5).then_inc(exp_done, 1)
            for i in range(NC - 1):
                act.wait_ge(prod_summed, NC + i)
                nc.scalar.activation(x1[:, i], ps[:, SUMS[(i + 1) % 2], 0:H], ACT.Copy).then_inc(x1_out, 1)
            for half in range(2):
                affine(half)
            for half in range(2):
                affine(half, "t_ln1_w", "t_ln1_b")
                for pair in range(2):
                    act.wait_ge(f1_done, 2 * half + pair + 1)
                    for m in (2 * pair, 2 * pair + 1):
                        nc.scalar.activation(f1_T[:, m, HALF[half]], ps[:, pair, (m % 2) * NH:(m % 2 + 1) * NH], ACT.Relu,
                                             bias=col("f1_b", m)).then_inc(f1_relu, 1)
            for half in range(2):
                affine(half, "t_ln2_w", "t_ln2_b")
            for c in range(NC):
                act.wait_ge(rz_ready, c + 1)
                nc.scalar.activation(rz[:, c], rz[:, c], ACT.Sigmoid).then_inc(rz_sig, 1)
                if c:
                    act.wait_ge(cand_ready, c)
                    nc.scalar.activation(cand[:, c - 1], cand[:, c - 1], ACT.Tanh).then_inc(cand_tanh, 1)
            act.wait_ge(cand_ready, NC)
            nc.scalar.activation(cand[:, NC - 1], cand[:, NC - 1], ACT.Tanh).then_inc(cand_tanh, 1)

        @block.vector
        def _(dve):
            W0, W1, W2 = (0, KE * H), (KE * H, (KE + KH) * H), ((KE + KH) * H, (KE + 2 * KH) * H)

            def split_x(par, count_hi, landed, freed):
                dve.wait_ge(x_loaded[par], landed)
                wait(dve, l0_done, freed)
                nc.vector.tensor_copy(x_hi[:, par], x_raw[:, par]).then_inc(x_hi_done, 1)

            def rest_x(par, half, hi):
                dve.wait_ge(x_hi_done, hi)
                ks = slice(2 * half, 2 * half + 2)
                nc.vector.tensor_tensor(x_lo[:, par, ks], x_raw[:, par, ks], x_hi[:, par, ks].bitcast(F32),
                                        ALU.subtract).then_inc(x_lo_done, 1)

            nc.vector.memset(count[:], 0.0).then_inc(count_step, 1)
            for n, (lo, hi) in enumerate((W0, W1, W2)):
                dve.wait_ge(w_loaded, 48)
                nc.vector.tensor_copy(w_hi[:, lo:hi], w_raw[:, lo:hi]).then_inc(w_hi_done, 1)
                if n == 0:
                    split_x(0, 1, 16, 0)
                dve.wait_ge(w_hi_done, n + 1)
                nc.vector.tensor_tensor(w_lo[:, lo:hi], w_raw[:, lo:hi], w_hi[:, lo:hi].bitcast(F32),
                                        ALU.subtract).then_inc(w_split, 1)
                if n == 0:
                    rest_x(0, 0, 1)
                    rest_x(0, 1, 1)
            dve.wait_ge(idx_loaded, 32)
            dve.wait_ge(iota_ready, 1)
            nc.vector.tensor_copy(iota[:], iota_i[:]).then_inc(idx_step, 1)
            nc.vector.tensor_copy(dst_f[:], dst_i[:]).then_inc(idx_step, 1)
            nc.vector.tensor_copy(src_f[:], src_i[:]).then_inc(idx_step, 1)
            dve.wait_ge(idx_step, 3)
            nc.vector.tensor_scalar(src_far[:], src_f[:], float(N // 2), None, ALU.is_ge).then_inc(idx_step, 1)
            dve.wait_ge(idx_step, 4)
            nc.vector.scalar_tensor_tensor(src_in[:], src_far[:], -float(N // 2), src_f[:], ALU.mult,
                                           ALU.add).then_inc(idx_step, 1)
            nc.vector.tensor_scalar(src_unit[:], src_far[:], float((1 << PACK_BITS) - 1), 1.0, ALU.mult,
                                    ALU.add).then_inc(idx_step, 1)
            dve.wait_ge(idx_step, 6)
            dve.wait_ge(m2b_loaded, 16)

            def hot(it, t):
                wait(dve, tile_summed, it.count(4, t - 7))
                at = bass.ds(it.count(4, t), 1)
                nc.vector.tensor_scalar(dst_hot[:, it.par, t], iota[:], dst_f[:, at], None, ALU.is_equal)
                nc.vector.tensor_scalar(pack_hot[:, it.par, t], iota[:, 0:2 * P], src_in[:, at], src_unit[:, at],
                                        ALU.is_equal, ALU.mult)
                nc.vector.tensor_scalar(src_hot[:, it.par, t], iota[:], src_f[:, at], None,
                                        ALU.is_equal).then_inc(hot_ready, 1)

            def rest(it, m, gelu, x, hi, lo, signal, back=0):
                dve.wait_ge(gelu, it.count(2, m + 1 - 2 * back))
                nc.vector.tensor_tensor(lo[:, m], x[:, m], hi[:, m].bitcast(F32), ALU.subtract).then_inc(signal, 1)

            def unpack(it, r):
                dve.wait_ge(count_out, it.windows(2, r - 1))
                dve.wait_ge(count_step, it.windows(8, 4 * r - 7))
                nc.vector.tensor_scalar(part[:, 0], packed[:, r], (1 << PACK_BITS) - 1, None,
                                        ALU.bitwise_and).then_inc(count_step, 1)
                nc.vector.tensor_scalar(part[:, 1], packed[:, r], PACK_BITS, None,
                                        ALU.logical_shift_right).then_inc(count_step, 1)
                for q in range(2):
                    dve.wait_ge(count_step, it.windows(8, 4 * r + q - 6))
                    s = 2 * q + r
                    nc.vector.tensor_tensor(count[:, s], count[:, s], part[:, q], ALU.add).then_inc(count_step, 1)

            def edge(it):
                nxt = 1 - it.par
                more = it.rnd is not None or it.b + 1 < NBLK
                counted = it.phase == 1 and (it.rnd is not None or it.b >= WINDOW)
                if it.has(1):
                    for h in range(2):
                        dve.wait_ge(l2_done, it.count(2, h - 1))
                        wait(dve, gelu2, it.count(2, h - 3))
                        nc.vector.tensor_tensor(m2_in[:, h], ps[:, (2 - bank0(it)) + h], m2b[:].rearrange("p a f -> p (a f)"),
                                                ALU.add).then_inc(m2_biased, 1)
                if more:
                    landed = 16 * ((it.b + 1) // 2 + 1)
                    if it.rnd is not None:
                        landed = it.rnd * (16 * WINDOW // 2) + landed
                    split_x(nxt, None, landed, it.count(2, 0))
                if it.has(1):
                    rest(it, 0, gelu2, m2, m2_hi, m2_lo, lo2_done, 1)
                if more:
                    rest_x(nxt, 0, it.count(1, 2))
                if it.has(1):
                    rest(it, 1, gelu2, m2, m2_hi, m2_lo, lo2_done, 1)
                if counted:
                    unpack(it, 0)
                if it.has():
                    rest(it, 0, gelu0, m0, m0_hi, m0_lo, lo0_done)
                    if more:
                        rest_x(nxt, 1, it.count(1, 2))
                    hot(it, 0)
                    rest(it, 1, gelu0, m0, m0_hi, m0_lo, lo0_done)
                    hot(it, 1)
                    hot(it, 2)
                    rest(it, 0, gelu1, m1, m1_hi, m1_lo, lo1_done)
                    hot(it, 3)
                    rest(it, 1, gelu1, m1, m1_hi, m1_lo, lo1_done)
                if counted:
                    unpack(it, 1)

            iterations(dve, edge)

            steps = [0]

            def step(ins):
                steps[0] += 1
                ins.then_inc(dve_step, 1)
                return steps[0]

            def link(ins):
                dve.wait_ge(dve_step, step(ins))

            def moments(chunks):
                cs = slice(chunks[0], chunks[-1] + 1)
                for c in chunks:
                    ins = nc.vector.bn_aggr(mean_var[:, c], stats[:, c])
                link(ins)
                link(nc.vector.tensor_scalar(half_var[:, cs], mean_var[:, cs, 1], LN_EPS, 0.5, ALU.add, ALU.mult))
                link(nc.vector.tensor_scalar(rstd[:, cs].bitcast(I32), half_var[:, cs].bitcast(I32), -0.5,
                                             float(RSQRT_SEED), ALU.mult, ALU.add))
                for _ in range(3):
                    for c in chunks:
                        one = slice(c, c + 1)
                        ins = nc.vector.scalar_tensor_tensor(sq[:, one], rstd[:, one], half_var[:, one], rstd[:, one],
                                                             ALU.mult, ALU.mult)
                    link(ins)
                    link(nc.vector.scalar_tensor_tensor(rstd[:, cs], sq[:, cs], 1.5, rstd[:, cs], ALU.subtract, ALU.mult,
                                                        reverse0=True))

            def normed(src, out, c):
                return nc.vector.tensor_scalar(out[:, c], src[:, c], mean_var[:, c, 0:1], rstd[:, c:c + 1],
                                               ALU.subtract, ALU.mult)

            def sums_and_stats(chunks, done, product, add):
                written = []
                for c in chunks:
                    dve.wait_ge(done, c + 1)
                    written.append(step(nc.vector.tensor_tensor(res[:, c], product(c), add[:, c], ALU.add)))
                for c, at in zip(chunks, written):
                    dve.wait_ge(dve_step, at)
                    ins = nc.vector.bn_stats(stats[:, c], res[:, c])
                link(ins)

            def norm(half, done, product, add):
                sums_and_stats(CHUNKS[half], done, product, add)
                moments(CHUNKS[half])
                hats_written(half, lambda c: normed(res, hat, c))

            hats = [0]

            def hats_written(half, one):
                for c in CHUNKS[half]:
                    one(c).then_inc(hat_ready, 1)
                hats[0] += len(CHUNKS[half])

            def rows_after(half, weight, bias, add, hat_count):
                dve.wait_ge(hat_ready, hat_count)
                cs = slice(2 * half, 2 * half + 2)
                out = skip if add else h_rows
                link(nc.vector.tensor_tensor(out[:, cs], hat[:, cs], row_half(row(weight)), ALU.mult))
                nc.vector.tensor_tensor(out[:, cs], out[:, cs], row_half(add if add else row(bias)), ALU.add).then_inc(skip_ready, 1)
                skips[0] += 1

            skips = [0]

            def rest_d1w(m):
                dve.wait_ge(d1w_hi_done, m + 1)
                nc.vector.tensor_tensor(d1w_lo[:, m % 2], d1_w[:, :, m * P:(m + 1) * P], d1w_hi[:, m % 2].bitcast(F32),
                                        ALU.subtract).then_inc(d1w_split, 1)

            def rest_gelu(i, n, hi, lo):
                dve.wait_ge(gelu_out, i + 1)
                nc.vector.tensor_tensor(lo, d_T[:, i % 4, 0:n], hi.bitcast(F32), ALU.subtract).then_inc(gelu_split, 1)

            dve.wait_ge(tile_summed, E // P)
            for m in range(KH):
                nc.vector.tensor_scalar(sum_T[:, m], ps[:, SUM + m], 1.0 / 30.0, None, ALU.mult).then_inc(sum_scaled, 1)
            dve.wait_ge(early_loaded, 48)
            for half in range(2):
                norm(half, sum_turned, sum_rows, x_rows)
            rest_d1w(0)
            rest_d1w(1)
            for r in range(2):
                unpack(Iteration(NBLK), r)
            for i in range(2 * KD):
                half, m = divmod(i, KD)
                rest_gelu(i, NH, d0_hi[:, m, HALF[half]], d0_lo[:, m, HALF[half]])
            dve.wait_ge(rows_loaded, 16)
            dve.wait_ge(bias_sums, 4)
            rows_after(0, "ln1_g", None, bias_row(0), hats[0])
            rows_after(1, "ln1_g", None, bias_row(0), hats[0])
            link(nc.vector.tensor_tensor(skip2[:], x_rows[:], row_all("ln2_b"), ALU.add))
            for m in range(KD):
                rest_gelu(2 * KD + m, N, d1_hi[:, m], d1_lo[:, m])
                if m + 2 < KD:
                    rest_d1w(m + 2)
                if m in (3, 4):
                    dve.wait_ge(d2w_hi_done, m - 2)
                    ks = slice((m - 3) * 4, (m - 3) * 4 + 4)
                    nc.vector.tensor_tensor(d2w_lo[:, ks], d2_w[:, ks], d2w_hi[:, ks].bitcast(F32),
                                            ALU.subtract).then_inc(d2w_split, 1)
            dve.wait_ge(skip_ready, skips[0])

            def between_norms(chunks):
                marks = [step(nc.vector.scalar_tensor_tensor(res[:, c], res[:, c], mean_var[:, c, 0:1], row("ln2_g"),
                                                             ALU.subtract, ALU.mult)) for c in chunks]
                for i, c in enumerate(chunks):
                    dve.wait_ge(dve_step, marks[i])
                    marks[i] = step(nc.vector.scalar_tensor_tensor(res[:, c], res[:, c], rstd[:, c:c + 1], skip2[:, c],
                                                                   ALU.mult, ALU.add))
                for i, c in enumerate(chunks):
                    dve.wait_ge(dve_step, marks[i])
                    ins = nc.vector.bn_stats(stats[:, c], res[:, c])
                link(ins)

            sums_and_stats(CHUNKS[0], d2_done, product_rows, skip)
            moments(CHUNKS[0])
            between_norms(CHUNKS[0])
            sums_and_stats(CHUNKS[1], d2_done, product_rows, skip)
            moments(range(NC))
            hats_written(0, lambda c: normed(res, xp, c))
            between_norms(CHUNKS[1])
            moments(CHUNKS[1])
            hats_written(1, lambda c: normed(res, xp, c))
            dve.wait_ge(hat_ready, hats[0])
            link(nc.vector.tensor_tensor(skip[:], xp[:], row_all("O_b"), ALU.add))
            pairs = [P, HEADS, HEADS, DH]
            SPLIT = NC - 1

            def score_products(c):
                dve.wait_ge(qkv_out, 2 * c + 2)
                if c >= 2:
                    dve.wait_ge(prod_summed, c - 1)
                q = qk_rows[:, c, 0:H].rearrange("p (h a d) -> p h a d", h=HEADS, a=1).to_broadcast(pairs)
                k = qk_rows[:, c, H:2 * H].rearrange("p (a g d) -> p a g d", a=1, g=HEADS).to_broadcast(pairs)
                view = prod[:, c % 2].rearrange("p (d h g) -> p h g d", h=HEADS, g=HEADS)
                ins = nc.vector.tensor_tensor(view, q, k, ALU.mult)
                if c < SPLIT:
                    ins.then_inc(prod_ready, 1)
                else:
                    link(ins)

            def score_sums(c):
                dve.wait_ge(prod_summed, c + 1)
                part_sums = ps[:, SUMS[c % 2], 0:H].rearrange("p (d r) -> p r d", d=4)
                nc.vector.tensor_reduce(probs[:, c].rearrange("p h g -> p (h g)"), part_sums, AX_X,
                                        ALU.add).then_inc(score_read, 1)

            score_products(0)
            score_products(1)
            score_sums(0)
            score_products(2)
            score_sums(1)
            score_products(3)
            link(nc.vector.tensor_reduce(probs[:, 3].rearrange("p h g -> p (h g)"),
                                         prod[:, 1].rearrange("p (d r) -> p r d", d=DH), AX_X, ALU.add))
            score_sums(2)
            dve.wait_ge(score_read, SPLIT)
            flat = probs[:].rearrange("p c h g -> p (c h) g")

            def each_g(t):
                return t[:].rearrange("p (r a) -> p r a", a=1).to_broadcast([P, NC * HEADS, HEADS])

            link(nc.vector.tensor_reduce(top[:], flat, AX_X, ALU.max))
            nc.vector.tensor_tensor(flat, flat, each_g(top), ALU.subtract).then_inc(scores_ready, 1)
            dve.wait_ge(exp_done, 1)
            link(nc.vector.tensor_reduce(total[:], flat, AX_X, ALU.add))
            link(nc.vector.reciprocal(total[:], total[:]))
            link(nc.vector.tensor_tensor(flat, flat, each_g(total), ALU.mult))
            for c in range(SPLIT):
                dve.wait_ge(prod_summed, max(SPLIT, SPLIT + c - 1))
                sm = probs[:, c].rearrange("p h (g a) -> p g h a", a=1).to_broadcast(pairs)
                v = v_rows[:, c].rearrange("p (g a d) -> p g a d", a=1, g=HEADS).to_broadcast(pairs)
                nc.vector.tensor_tensor(prod[:, c % 2].rearrange("p (g h d) -> p g h d", h=HEADS, g=HEADS), sm, v,
                                        ALU.mult).then_inc(prod_ready, 1)
            dve.wait_ge(prod_summed, SPLIT + 2)
            sm = probs[:, 3].rearrange("p h (a g) -> p h a g", a=1).to_broadcast([P, HEADS, DH, HEADS])
            v = v_rows[:, 3].rearrange("p (a g d) -> p a d g", a=1, g=HEADS).to_broadcast([P, HEADS, DH, HEADS])
            view = prod[:, 1].rearrange("p (h d g) -> p h d g", h=HEADS, d=DH)
            link(nc.vector.tensor_tensor(view, sm, v, ALU.mult))
            nc.vector.tensor_reduce(x1[:, 3].rearrange("p (h d) -> p h d", h=HEADS), view, AX_X,
                                    ALU.add).then_inc(x1_ready, 1)
            dve.wait_ge(x1_ready, 1)
            dve.wait_ge(x1_out, SPLIT)
            for half in range(2):
                dve.wait_ge(gathered, half + 1)
                hats_written(half, lambda c: nc.vector.tensor_tensor(hat[:, c], x1[:, c], product_rows(c), ALU.mult))
            for half in range(2):
                norm(half, o_done, product_rows, skip)
                rows_after(half, "t_ln1_w", None, bias_row(1), hats[0])
            for half in range(2):
                dve.wait_ge(skip_ready, skips[0])
                norm(half, f2_done, product_rows, skip)
                rows_after(half, "t_ln2_w", "t_ln2_b", None, hats[0])
            dve.wait_ge(skip_ready, skips[0])
            dve.wait_ge(bias_sums, 7)

            def gates_in(c):
                dve.wait_ge(gru_done, c + 1)
                bank = GRU_BANKS[c]
                nc.vector.tensor_tensor(rz[:, c], ps[:, bank], b_rz[:], ALU.add).then_inc(rz_ready, 1)
                nc.vector.tensor_tensor(gn[:, c], ps[:, bank + 1], b_n[:], ALU.add).then_inc(gn_ready, 1)

            def candidate_in(c):
                dve.wait_ge(gn_ready, c + 1)
                dve.wait_ge(rz_sig, c + 1)
                link(nc.vector.tensor_tensor(gn[:, c, H:2 * H], gn[:, c, H:2 * H], rz[:, c, 0:H], ALU.mult))
                nc.vector.tensor_tensor(cand[:, c], gn[:, c, 0:H], gn[:, c, H:2 * H], ALU.add).then_inc(cand_ready, 1)

            def gru_out(c):
                dve.wait_ge(cand_tanh, c + 1)
                nc.vector.tensor_tensor(gn[:, c, 0:H], xp[:, c], cand[:, c], ALU.add)
                link(nc.vector.tensor_tensor(res[:, c], h_rows[:, c], cand[:, c], ALU.subtract))
                link(nc.vector.tensor_tensor(res[:, c], res[:, c], rz[:, c, H:2 * H], ALU.mult))
                link(nc.vector.tensor_tensor(res[:, c], res[:, c], gn[:, c, 0:H], ALU.add))
                nc.vector.bn_stats(stats[:, c], res[:, c]).then_inc(dve_step, 1)
                steps[0] += 1

            def last_norm(half):
                dve.wait_ge(dve_step, steps[0])
                moments(CHUNKS[half])
                for c in CHUNKS[half]:
                    normed(res, hat, c).then_inc(out_ready, 1)

            for i in range(NC + 2):
                if i < NC:
                    gates_in(i)
                if 1 <= i < NC + 1:
                    candidate_in(i - 1)
                if i >= 2:
                    gru_out(i - 2)
                if i == 3:
                    last_norm(0)
            last_norm(1)

        @block.tensor
        def _(pe):
            def w(n, k, m, part):
                at = ((0, KE, KE + KH)[n] + k) * H
                return part[:, at + m * P:at + (m + 1) * P]

            def passes(a_hi, a_lo, b_hi, b_lo):
                return (a_hi, b_hi), (a_hi, b_lo), (a_lo, b_hi)

            def layer(it, n, bank, hi, lo, chunks, free, free_count, in_ready, in_count, done):
                for m in range(KH):
                    wait(pe, free, it.count(*free_count(m)))
                    for k in range(chunks):
                        if m == 0:
                            for s, value in in_ready(k):
                                pe.wait_ge(s, value)
                        ops = passes(w(n, k, m, w_hi), w(n, k, m, w_lo), hi[:, k], lo[:, k])
                        for i, (a, b) in enumerate(ops):
                            last = nc.tensor.matmul(ps[:, bank + m], a, b, start=(k == 0 and i == 0),
                                                    stop=(k == chunks - 1 and i == 2))
                    last.then_inc(done, 1)

            def sum_tile(it, t):
                par = 1 - it.par
                pe.wait_ge(hot_ready, it.count(4, t - 3))
                pe.wait_ge(lo2_done, it.count(2, t // 2 - 1))
                lone = it.rnd is None
                first, final = lone and it.b == 1 and t == 0, lone and it.b == NBLK and t == TB - 1
                phase = (it.phase - 1) % WINDOW
                if phase == 0 and t == 0 and not first:
                    pe.wait_ge(count_out, it.windows(2, 0))
                half, at = t // 2, (t % 2) * H
                for m in range(KH):
                    for i, part in enumerate((m2_hi, m2_lo)):
                        nc.tensor.matmul(ps[:, SUM + m], part[:, half, at + m * P:at + (m + 1) * P], src_hot[:, par, t],
                                         start=(first and i == 0), stop=(final and i == 1), skip_group_check=True)
                for r in range(2):
                    last = nc.tensor.matmul(ps[:, CNT + r], pack_hot[:, par, t, r * P:(r + 1) * P], dst_hot[:, par, t],
                                            start=(phase == 0 and t == 0), stop=(phase == WINDOW - 1 and t == TB - 1),
                                            skip_group_check=True)
                last.then_inc(tile_summed, 1)

            def messages(it):
                for t in range(TB):
                    h = t // 2
                    if t % 2 == 0:
                        pe.wait_ge(gelu0, it.count(2, h + 1))
                    if t == 0:
                        pe.wait_ge(lo1_done, it.count(2, 2))
                    out = ps[:, bank0(it) + h, (t % 2) * H:(t % 2 + 1) * H]
                    for k in range(KH):
                        e = slice(t * P, (t + 1) * P)
                        at = (KE + KH + k) * H
                        ops = passes(m1_hi[:, k, e], m1_lo[:, k, e], w_hi[:, at:at + H], w_lo[:, at:at + H])
                        for i, (a, b) in enumerate(ops):
                            last = nc.tensor.matmul(out, a, b, start=(k == 0 and i == 0), stop=(k == KH - 1 and i == 2))
                    if t % 2:
                        last.then_inc(l2_done, 1)

            def edge(it):
                if it.has():
                    if it.first():
                        pe.wait_ge(w_split, 1)
                    layer(it, 0, bank0(it), x_hi[:, it.par], x_lo[:, it.par], KE, gelu1, lambda m: (2, m - 1),
                          lambda k: [(x_lo_done, it.count(2, k // 2 + 1))] if k % 2 == 0 else [], None, l0_done)
                if it.has(1):
                    sum_tile(it, 0)
                    sum_tile(it, 1)
                if it.has():
                    if it.first():
                        pe.wait_ge(w_split, 3)
                    layer(it, 1, bank1(it), m0_hi, m0_lo, KH, m2_biased, lambda m: (2, m - 1),
                          lambda k: [(lo0_done, it.count(2, k + 1))], None, l1_done)
                if it.has(1):
                    sum_tile(it, 2)
                    sum_tile(it, 3)
                if it.has():
                    messages(it)

            iterations(pe, edge)

            def turn(src, k, c, out):
                return nc.tensor.transpose(out, src, ident[:])

            pe.wait_ge(sum_scaled, 2)
            pe.wait_ge(ident_ready, 1)
            for c in range(NC):
                if c == NC // 2:
                    pe.wait_ge(count_out, 2 * (NBLK // WINDOW))
                for m in range(KH):
                    last = nc.tensor.transpose(sum_rows(c)[:, m * P:(m + 1) * P], sum_T[:, m, c * P:(c + 1) * P], ident[:])
                last.then_inc(sum_turned, 1)
            hats = [0]
            acts = [0]

            def turn_rows(src, half):
                for i, c in enumerate(CHUNKS[half]):
                    hats[0] += 1
                    pe.wait_ge(hat_ready, hats[0])
                    for k in range(KH):
                        last = nc.tensor.transpose(turned_bank(half, k)[:, i * P:(i + 1) * P], src[:, c, k * P:(k + 1) * P],
                                                   ident[:])
                last.then_inc(hat_turned, 1)
                acts[0] += KH
                return acts[0]

            def to_columns(weights, chunks, m, rhs, half, out):
                for k in range(chunks):
                    last = nc.tensor.matmul(out, weights[:, k, m * P:(m + 1) * P], rhs[:, k, HALF[half]], start=(k == 0),
                                            stop=(k == chunks - 1))
                return last

            def to_rows(lhs, chunks, weights, half, done):
                for c in CHUNKS[half]:
                    for k in range(chunks):
                        last = nc.tensor.matmul(product_rows(c), lhs[:, k, c * P:(c + 1) * P], weights[:, k],
                                                start=(k == 0), stop=(k == chunks - 1))
                    last.then_inc(done, 1)

            pe.wait_ge(early_loaded, 48)
            turned = [turn_rows(hat, 0), None]
            for i in range(2 * KD):
                half, m = divmod(i, KD)
                if i == 2:
                    turned[1] = turn_rows(hat, 1)
                if m == 0:
                    pe.wait_ge(act_ready, turned[half])
                if i >= 4:
                    pe.wait_ge(gelu_out, i - 3)
                to_columns(d0_w, KH, m, act_T, half, ps[:, 4 + m % 4, 0:NH]).then_inc(d0_done, 1)
            for m in range(KD):
                if m >= 4:
                    pe.wait_ge(gelu_out, 2 * KD + m - 3)
                pe.wait_ge(d1w_split, m + 1)
                for k in range(KD):
                    if m == 0:
                        pe.wait_ge(gelu_split, KD + k + 1)
                    ops = passes(d1w_hi[:, m % 2, k], d1w_lo[:, m % 2, k], d0_hi[:, k], d0_lo[:, k])
                    for i, (a, b) in enumerate(ops):
                        last = nc.tensor.matmul(ps[:, m % 4], a, b, start=(k == 0 and i == 0),
                                                stop=(k == KD - 1 and i == 2))
                last.then_inc(d1_done, 1)
            pe.wait_ge(d2w_split, 2)
            for c in range(NC):
                for k in range(KD):
                    if c == 0:
                        pe.wait_ge(gelu_split, 2 * KD + k + 1)
                    e = slice(c * P, (c + 1) * P)
                    ops = passes(d1_hi[:, k, e], d1_lo[:, k, e], d2w_hi[:, k], d2w_lo[:, k])
                    for i, (a, b) in enumerate(ops):
                        last = nc.tensor.matmul(product_rows(c), a, b, start=(k == 0 and i == 0),
                                                stop=(k == KD - 1 and i == 2))
                last.then_inc(d2_done, 1)
            for c in range(NC):
                if c % 2 == 0:
                    pe.wait_ge(act_ready, turn_rows(xp, c // 2))
                    pe.wait_ge(second_loaded, SECOND)
                if c >= 2:
                    pe.wait_ge(qkv_out, 2 * c - 2)
                for bank, weights, width in ((c % 2, wqk, 2 * H), (4 + c % 2, wv, H)):
                    for k in range(KH):
                        last = nc.tensor.matmul(ps[:, bank, 0:width], act_T[:, k, c * P:(c + 1) * P], weights[:, k],
                                                start=(k == 0), stop=(k == KH - 1))
                last.then_inc(qkv_done, 1)
            for i in range(2 * (NC - 1)):
                pe.wait_ge(prod_ready, i + 1)
                if i in (2, 3, 4):
                    pe.wait_ge(score_read, i - 1)
                if i == 5:
                    pe.wait_ge(x1_out, 1)
                c = i % (NC - 1)
                for j in range(HEADS):
                    last = nc.tensor.matmul(ps[:, SUMS[i % 2], 0:H], ident[:], prod[:, c % 2, j * H:(j + 1) * H],
                                            start=(j == 0), stop=(j == HEADS - 1))
                last.then_inc(prod_summed, 1)
            pe.wait_ge(count_step, 1 + 8 * (NBLK // WINDOW))
            for s in range(NC):
                if s < NC - 1:
                    pe.wait_ge(x1_out, s + 1)
                else:
                    pe.wait_ge(x1_ready, 1)
                for c in range(NC):
                    last = nc.tensor.matmul(product_rows(c), count[:, s, c * P:(c + 1) * P], x1[:, s], start=(s == 0),
                                            stop=(s == NC - 1))
                    if s == NC - 1 and c % 2:
                        last.then_inc(gathered, 1)
            for half in range(2):
                pe.wait_ge(act_ready, turn_rows(hat, half))
                to_rows(act_T, KH, wo, half, o_done)
            for half in range(2):
                pe.wait_ge(act_ready, turn_rows(hat, half))
                for pair in range(2):
                    for m in (2 * pair, 2 * pair + 1):
                        last = to_columns(f1_w, KH, m, act_T, half, ps[:, pair, (m % 2) * NH:(m % 2 + 1) * NH])
                    last.then_inc(f1_done, 1)
                for c in CHUNKS[half]:
                    for k in range(4):
                        if c == CHUNKS[half][0]:
                            pe.wait_ge(f1_relu, 4 * half + k + 1)
                        last = nc.tensor.matmul(product_rows(c), f1_T[:, k, c * P:(c + 1) * P], f2_w[:, k],
                                                start=(k == 0), stop=(k == 3))
                    last.then_inc(f2_done, 1)
            pe.wait_ge(rz_weights, 1)
            for c in range(NC):
                if c % 2 == 0:
                    pe.wait_ge(act_ready, turn_rows(hat, c // 2))
                if GRU_BANKS[c] in GRU_BANKS[:c]:
                    before = GRU_BANKS.index(GRU_BANKS[c])
                    pe.wait_ge(rz_ready, before + 1)
                    pe.wait_ge(gn_ready, before + 1)
                bank = GRU_BANKS[c]
                for k in range(KH):
                    nc.tensor.matmul(ps[:, bank], act_T[:, k, c * P:(c + 1) * P], w_rz[:, k], start=(k == 0),
                                     stop=(k == KH - 1))
                for at, wn in ((0, w_ih), (H, w_hh)):
                    for k in range(KH):
                        last = nc.tensor.matmul(ps[:, bank + 1, at:at + H], act_T[:, k, c * P:(c + 1) * P],
                                                wn[:, k, 2 * H:3 * H], start=(k == 0), stop=(k == KH - 1))
                last.then_inc(gru_done, 1)


def kernel(**inputs):
    import numpy as np
    import concourse.bacc as bacc
    from concourse.bass_utils import run_bass_kernel_spmd

    a = {k: np.asarray(v) for k, v in inputs.items()}

    def chunked(w):
        return np.ascontiguousarray(w.reshape(-1, P, w.shape[1]).transpose(1, 0, 2).reshape(P, -1))

    L0, L1 = "L0_gnn_", "L1_gnn_"
    col_src = {"m0_b": L0 + "m0_b", "m1_b": L0 + "m1_b", "ln1_g": L0 + "ln1_g", "ln1_b": L0 + "ln1_b",
               "d0_b": L0 + "d0_b", "d1_b": L0 + "d1_b", "t_ln1_w": L1 + "ln1_w", "t_ln1_b": L1 + "ln1_b",
               "f1_b": L1 + "f1_b", "t_ln2_w": L1 + "ln2_w", "t_ln2_b": L1 + "ln2_b"}
    row_src = {"ln1_g": L0 + "ln1_g", "ln1_b": L0 + "ln1_b", "d2_b": L0 + "d2_b", "ln2_g": L0 + "ln2_g",
               "ln2_b": L0 + "ln2_b", "O_b": L1 + "O_b", "t_ln1_w": L1 + "ln1_w", "t_ln1_b": L1 + "ln1_b",
               "f2_b": L1 + "f2_b", "t_ln2_w": L1 + "ln2_w", "t_ln2_b": L1 + "ln2_b", "b_ih": L1 + "gru_b_ih",
               "b_hh": L1 + "gru_b_hh"}
    data = [
        ("x_rows", chunked(a["x"])),
        ("edges", np.ascontiguousarray(a["edge_attr_512"].reshape(NBLK, BLK, KE, P).transpose(0, 3, 2, 1)
                                       .reshape(NBLK, P, KE * BLK))),
        ("src", np.ascontiguousarray(a["src"].reshape(E // P, P).T)),
        ("dst", np.ascontiguousarray(a["dst"].reshape(E // P, P).T)),
        ("w0", chunked(a[L0 + "m0_w"])), ("w1", chunked(a[L0 + "m1_w"])), ("w2", chunked(a[L0 + "m2_w"])),
        ("m2b", np.concatenate([a[L0 + "m2_b"]] * 2).reshape(1, 2 * H)),
        ("cols", np.ascontiguousarray(np.concatenate([a[col_src[n]].reshape(-1, P) for n in COLS]).T)),
        ("rows", np.concatenate([a[row_src[n]] for n in ROWS]).reshape(1, NROWS)),
        ("d0", chunked(a[L0 + "d0_w"])), ("d1", chunked(a[L0 + "d1_w"])), ("d2", chunked(a[L0 + "d2_w"])),
        ("wqk", chunked(np.concatenate([a[L1 + "Wq"], a[L1 + "Wk"]], axis=1))), ("wv", chunked(a[L1 + "Wv"])),
        ("wo", chunked(a[L1 + "O_w"])), ("f1", chunked(a[L1 + "f1_w"])), ("f2", chunked(a[L1 + "f2_w"])),
        ("wih", chunked(a[L1 + "gru_w_ih"])), ("whh", chunked(a[L1 + "gru_w_hh"])),
    ]
    nc = bacc.Bacc("TRN2", target_bir_lowering=False, num_devices=1)
    aps = [nc.dram_tensor(f"in_{n}_dram", v.shape, mybir.dt.from_np(v.dtype), kind="ExternalInput").ap() for n, v in data]
    out = nc.dram_tensor("out_dram", (NC, P, H), F32, kind="ExternalOutput").ap()
    gnn_kernel(nc, *aps, out)
    result = run_bass_kernel_spmd(nc, [{f"in_{n}_dram": v for n, v in data}], core_ids=[0])
    return result.results[0]["out_dram"].reshape(N, H)
```

```python
from contextlib import ExitStack

import concourse.bass as bass
from concourse import mybir

F32 = mybir.dt.float32
F32R = mybir.dt.float32r
BF16 = mybir.dt.bfloat16
FP16 = mybir.dt.float16
I32 = mybir.dt.int32
ALU = mybir.AluOpType
ACT = mybir.ActivationFunctionType
AX_X = mybir.AxisListType.X

P = 128
N = 512
H = 256
E = 16384
EIN = 512
D = 1024
HEADS = 8
DH = H // HEADS
BLK = 512
TB = BLK // P
NBLK = E // BLK
KE = EIN // P
KH = H // P
KD = D // P
NC = N // P
LN_EPS = 1e-5
WINDOW = 4
PACK_BITS = 12
RSQRT_SEED = 0x5F3759DF - (1 << 22)

COLS = {}
_at = 0
for _name, _n in (("m0_b", KH), ("m1_b", KH), ("ln1_g", KH), ("ln1_b", KH), ("d0_b", KD), ("d1_b", KD),
                  ("t_ln1_w", KH), ("t_ln1_b", KH), ("f1_b", 4), ("t_ln2_w", KH), ("t_ln2_b", KH)):
    COLS[_name] = (_at, _n)
    _at += _n
NCOLS = _at
ROWS = {}
_at = 0
for _name, _n in (("ln1_g", H), ("ln1_b", H), ("d2_b", H), ("ln2_g", H), ("ln2_b", H), ("O_b", H),
                  ("t_ln1_w", H), ("t_ln1_b", H), ("f2_b", H), ("t_ln2_w", H), ("t_ln2_b", H),
                  ("b_ih", 3 * H), ("b_hh", 3 * H)):
    ROWS[_name] = (_at, _n)
    _at += _n
NROWS = _at


def gnn_kernel(nc, x_rows_d, edges_d, src_d, dst_d, w0_d, w1_d, w2_d, m2b_d, cols_d, rows_d, d0_d, d1_d, d2_d,
               wqk_d, wv_d, wo_d, f1_d, f2_d, wih_d, whh_d, out_d):
    ctx = ExitStack()
    with ctx:
        mem = [ctx]

        def sb(name, shape, dt=F32):
            return mem[0].enter_context(nc.sbuf_tensor(name, shape, dt))

        def sem(name):
            return ctx.enter_context(nc.semaphore(name))

        x_rows = sb("x_rows", [P, NC, H])
        cols = sb("cols", [P, NCOLS])
        d0_w = sb("d0_w", [P, KH, D])
        d1_w = sb("d1_w", [P, KD, D])
        count = sb("count", [P, NC, N])
        ident = sb("ident", [P, P])

        edge_mem = ExitStack()
        mem[0] = edge_mem
        w_raw = sb("w_raw", [P, (KE + 2 * KH) * H])
        w_hi = sb("w_hi", [P, (KE + 2 * KH) * H], F32R)
        w_lo = sb("w_lo", [P, (KE + 2 * KH) * H], F32R)
        m2b = sb("m2b", [P, 2, H])
        x_raw = sb("x_raw", [P, 2, KE, BLK])
        x_hi = sb("x_hi", [P, 2, KE, BLK], F32R)
        x_lo = sb("x_lo", [P, 2, KE, BLK], F32R)
        m0 = sb("m0", [P, KH, BLK])
        m0_hi = sb("m0_hi", [P, KH, BLK], F32R)
        m0_lo = sb("m0_lo", [P, KH, BLK], F32R)
        m1 = sb("m1", [P, KH, BLK])
        m1_hi = sb("m1_hi", [P, KH, BLK], F32R)
        m1_lo = sb("m1_lo", [P, KH, BLK], F32R)
        m2_in = sb("m2_in", [P, 2, 2 * H])
        m2 = sb("m2", [P, 2, 2 * H])
        m2_hi = sb("m2_hi", [P, 2, 2 * H], F32R)
        m2_lo = sb("m2_lo", [P, 2, 2 * H], F32R)
        src_hot = sb("src_hot", [P, 2, TB, N], F32R)
        dst_hot = sb("dst_hot", [P, 2, TB, N], BF16)
        pack_hot = sb("pack_hot", [P, 2, TB, 2 * P], BF16)
        iota_i = sb("iota_i", [P, N], I32)
        iota = sb("iota", [P, N], FP16)
        src_i = sb("src_i", [P, E // P], I32)
        dst_i = sb("dst_i", [P, E // P], I32)
        src_f = sb("src_f", [P, E // P])
        dst_f = sb("dst_f", [P, E // P])
        src_far = sb("src_far", [P, E // P])
        src_in = sb("src_in", [P, E // P])
        src_unit = sb("src_unit", [P, E // P])
        packed = w_raw[:, 0:2 * N].bitcast(I32).rearrange("p (r n) -> p r n", r=2)
        part = w_raw[:, 2 * N:4 * N].bitcast(I32).rearrange("p (r n) -> p r n", r=2)
        edge_mem.close()

        node_mem = ExitStack()
        mem[0] = node_mem
        rows = sb("rows", [P, NROWS])
        res = sb("res", [P, NC, H])
        hat = sb("hat", [P, NC, H])
        stats = sb("stats", [P, NC, 6])
        mean_var = sb("mean_var", [P, NC, 2])
        half_var = sb("half_var", [P, NC])
        rstd = sb("rstd", [P, NC])
        sq = sb("sq", [P, NC])
        h_rows = sb("h_rows", [P, NC, H])
        skip = sb("skip", [P, NC, H])
        skip2 = sb("skip2", [P, NC, H])
        xp = sb("xp", [P, NC, H])
        act_T = sb("act_T", [P, KH, N])
        bias_sum = sb("bias_sum", [P, 2, H])
        node_mlp_mem = ExitStack()
        mem[0] = node_mlp_mem
        d_T = sb("d_T", [P, 4, N])
        d0_hi = sb("d0_hi", [P, KD, N], F32R)
        d0_lo = sb("d0_lo", [P, KD, N], F32R)
        d1_hi = sb("d1_hi", [P, KD, N], F32R)
        d1_lo = sb("d1_lo", [P, KD, N], F32R)
        d1w_hi = sb("d1w_hi", [P, 2, KD, P], F32R)
        d1w_lo = sb("d1w_lo", [P, 2, KD, P], F32R)
        d2w_hi = sb("d2w_hi", [P, KD, H], F32R)
        d2w_lo = sb("d2w_lo", [P, KD, H], F32R)
        sum_T = d_T[:, 0:KH]
        d2_w = d0_w[:].rearrange("p k (j n) -> p (k j) n", n=H)
        node_mlp_mem.close()
        second_mem = ExitStack()
        mem[0] = second_mem
        prod2 = sb("prod2", [P, HEADS * HEADS * DH])
        wqk = sb("wqk", [P, KH, 2 * H])        
        wv = sb("wv", [P, KH, H])
        wo = sb("wo", [P, KH, H])
        f1_w = sb("f1_w", [P, KH, 2 * H])
        f2_w = sb("f2_w", [P, 4, H])
        w_ih = sb("w_ih", [P, KH, 3 * H])
        w_hh = sb("w_hh", [P, KH, 3 * H])
        w_rz = sb("w_rz", [P, KH, 2 * H])
        qk_rows = sb("qk_rows", [P, NC, 2 * H])
        v_rows = sb("v_rows", [P, NC, H])
        prod01 = sb("prod01", [P, 2, HEADS * HEADS * DH])
        probs = sb("probs", [P, NC, HEADS, HEADS])
        top = sb("top", [P, NC * HEADS])
        total = sb("total", [P, NC * HEADS])
        x1 = sb("x1", [P, NC, H])
        b_gru = sb("b_gru", [P, 4 * H])
        b_gru_hi = sb("b_gru_hi", [P, 4 * H], F32R)
        b_gru_lo = sb("b_gru_lo", [P, 4 * H], F32R)
        ones = sb("ones", [P, P], F32R)
        cand = sb("cand", [P, NC, H])
        f1_T = sb("f1_T", [P, 4, N])
        prod = (prod01[:, 0], prod01[:, 1], prod2[:], f1_T[:].rearrange("p k n -> p (k n)"))
        rz = prod01[:, 0].rearrange("p (c n) -> p c n", c=NC)
        one_less_z = prod01[:, 1, 0:NC * H].rearrange("p (c f) -> p c f", c=NC)
        kept = prod01[:, 1, NC * H:].rearrange("p (c f) -> p c f", c=NC)
        second_mem.close()
        node_mem.close()
        mem[0] = ctx

        ps = ctx.enter_context(nc.psum_tensor("ps", [P, 8, 512], F32))
        SUM, CNT = 4, 6

        SCORE_BANK, OUT_BANK = (2, 6, 2), (0, 1, 3)
        GRU_BANKS = (0, 4, 6, 0)
        CHUNKS = (range(0, NC // 2), range(NC // 2, NC))
        NH = N // 2
        HALF = (slice(0, NH), slice(NH, N))

        def col(name, i):
            at, _ = COLS[name]
            return cols[:, at + i:at + i + 1]

        def span(name):
            at, size = ROWS[name]
            return at, at + size

        def row(name, lo=0, n=None):
            at, size = ROWS[name]
            return rows[:, at + lo:at + lo + (n or size)]

        def product_rows(c):
            return ps[:, 4 + c, 0:H]

        def sum_rows(c):
            return ps[:, (0, 1, CNT, CNT + 1)[c], 0:H]

        def turned_bank(half, k):
            return ps[:, 2 + half, k * NH:(k + 1) * NH]

        def row_half(r):
            return r.rearrange("p (a f) -> p a f", a=1).to_broadcast([P, NC // 2, H])

        def bias_row(i):
            return bias_sum[:, i]

        def row_all(name):
            return row(name).rearrange("p (a f) -> p a f", a=1).to_broadcast([P, NC, H])

        x_loaded = [sem("x_loaded0"), sem("x_loaded1")]
        x0_loaded = [sem("x0_loaded0"), sem("x0_loaded1")]
        w_loaded = [sem(f"w_loaded{g}") for g in range(4)]
        m2b_loaded, idx_loaded, x0_hi_done = sem("m2b_loaded"), sem("idx_loaded"), sem("x0_hi_done")
        cols_loaded, early_loaded, rows_loaded = sem("cols_loaded"), sem("early_loaded"), sem("rows_loaded")
        d2_loaded, second_loaded = sem("d2_loaded"), sem("second_loaded")
        iota_ready = sem("iota_ready")
        ident_zero, ident_ready = sem("ident_zero"), sem("ident_ready")
        w_hi_done, w_split = sem("w_hi_done"), sem("w_split")
        idx_step = sem("idx_step")
        x_hi_done, x_lo_done = sem("x_hi_done"), sem("x_lo_done")
        l0_done, l1_done, l2_done = sem("l0_done"), sem("l1_done"), sem("l2_done")
        gelu0, gelu1, gelu2 = sem("gelu0"), sem("gelu1"), sem("gelu2")
        lo0_done, lo1_done, lo2_done = sem("lo0_done"), sem("lo1_done"), sem("lo2_done")
        m2_biased = sem("m2_biased")
        hot_ready, tile_summed = sem("hot_ready"), sem("tile_summed")
        count_out, count_step = sem("count_out"), sem("count_step")
        sum_scaled, sum_turned = sem("sum_scaled"), sem("sum_turned")
        hat_ready, hat_turned, act_ready = sem("hat_ready"), sem("hat_turned"), sem("act_ready")
        skip_ready = sem("skip_ready")
        d0_done, d1_done, d2_done = sem("d0_done"), sem("d1_done"), sem("d2_done")
        gelu_out, gelu_split = sem("gelu_out"), sem("gelu_split")
        d1w_hi_done, d1w_split = sem("d1w_hi_done"), sem("d1w_split")
        d2w_hi_done, d2w_split = sem("d2w_hi_done"), sem("d2w_split")
        qkv_done, qkv_out = sem("qkv_done"), sem("qkv_out")
        scores_ready, exp_done = sem("scores_ready"), sem("exp_done")
        prod_ready, prod_summed = sem("prod_ready"), sem("prod_summed")
        x1_out, x1_ready, gathered = sem("x1_out"), sem("x1_ready"), sem("gathered")
        rz_weights = sem("rz_weights")
        bias_sums, b_hi_done, b_split = sem("bias_sums"), sem("b_hi_done"), sem("b_split")
        o_done, f1_done, f1_relu, f2_done = sem("o_done"), sem("f1_done"), sem("f1_relu"), sem("f2_done")
        gru_done, rz_sig = sem("gru_done"), sem("rz_sig")
        cand_ready, cand_tanh = sem("cand_ready"), sem("cand_tanh")
        out_ready, out_stored = sem("out_ready"), sem("out_stored")
        dve_step = sem("dve_step")

        W = [slice(g * KH * H, (g + 1) * KH * H) for g in range(4)]
        K_HALF = (slice(0, KE // 2), slice(KE // 2, KE))

        block = ctx.enter_context(nc.Block())

        def wait(eng, s, value):
            if not isinstance(value, int) or value > 0:
                eng.wait_ge(s, value)

        LEAD = 2
        ROUNDS = (NBLK - LEAD - 2) // WINDOW

        class Iteration:
            def __init__(self, b, rnd=None):
                self.b, self.rnd = b, rnd
                self.phase, self.par = b % WINDOW, b % 2

            def count(self, per_block, more=0):
                fixed = per_block * self.b + more
                return fixed if self.rnd is None else self.rnd * (WINDOW * per_block) + fixed

            def windows(self, per_window, more=0):
                fixed = per_window * (self.b // WINDOW) + more
                return fixed if self.rnd is None else self.rnd * per_window + fixed

            def first(self):
                return self.rnd is None and self.b == 0

            def has(self, back=0):
                return self.rnd is not None or 0 <= self.b - back < NBLK

        def iterations(eng, one):
            for b in range(LEAD):
                one(Iteration(b))
            with eng.Fori(0, ROUNDS) as rnd:
                for j in range(WINDOW):
                    one(Iteration(LEAD + j, rnd))
            for b in range(LEAD + ROUNDS * WINDOW, NBLK + 1):
                one(Iteration(b))

        def bank0(it):
            return 2 * it.par

        def bank1(it):
            return 2 - 2 * it.par

        @block.sync
        def _(sp):
            def load_x(b, par, split):
                wait(sp, x_lo_done, split)
                src = edges_d[b] if isinstance(b, int) else edges_d[bass.ds(b, 1)].rearrange("a p n -> p (a n)")
                sp.dma_start(x_raw[:, par].rearrange("p k e -> p (k e)"), src).then_inc(x_loaded[par], 16)

            for g, (ws, ks) in enumerate(zip(W[:2], K_HALF)):
                sp.dma_start(w_raw[:, ws], w0_d[:, ws]).then_inc(w_loaded[g], 16)
                sp.dma_start(x_raw[:, 0, ks].rearrange("p k e -> p (k e)"),
                             edges_d[0][:, ks.start * BLK:ks.stop * BLK]).then_inc(x0_loaded[g], 16)
            sp.dma_start(w_raw[:, W[2]], w1_d).then_inc(w_loaded[2], 16)
            sp.dma_start(w_raw[:, W[3]], w2_d).then_inc(w_loaded[3], 16)
            load_x(1, 1, 0)
            with sp.Fori(0, (NBLK - 2) // 2) as g:
                for par in range(2):
                    load_x(g * 2 + (2 + par), par, g * 4 + (2 + 2 * par))
            sp.dma_start(x_rows[:].rearrange("p c f -> p (c f)"), x_rows_d).then_inc(early_loaded, 16)
            sp.dma_start(d0_w[:].rearrange("p a b -> p (a b)"), d0_d).then_inc(early_loaded, 16)
            sp.dma_start(d1_w[:].rearrange("p a b -> p (a b)"), d1_d).then_inc(early_loaded, 16)
            sp.wait_ge(tile_summed, E // P)
            sp.wait_ge(count_step, 1 + 8 * (NBLK // WINDOW))
            sp.dma_start(rows[:], rows_d.to_broadcast([P, NROWS])).then_inc(rows_loaded, 16)
            sp.wait_ge(d0_done, 2 * KD)
            sp.dma_start(d2_w, d2_d.rearrange("p (a b) -> p a b", b=H)).then_inc(d2_loaded, 16)
            sp.wait_ge(d1_done, KD)
            for dst, src in ((wqk, wqk_d), (wv, wv_d), (w_ih, wih_d), (w_hh, whh_d), (wo, wo_d), (f1_w, f1_d), (f2_w, f2_d)):
                sp.dma_start(dst[:].rearrange("p a b -> p (a b)"), src).then_inc(second_loaded, 16)
            for c in range(NC):
                sp.wait_ge(out_ready, c + 1)
                sp.dma_start(out_d[c], hat[:, c]).then_inc(out_stored, 16)
            sp.wait_ge(out_stored, 16 * NC)

        SECOND = 16 * 7

        @block.gpsimd
        def _(pool):
            pool.memset(count[:], 0.0).then_inc(count_step, 1)
            pool.iota(iota_i[:], [[1, N]], base=0, channel_multiplier=0).then_inc(iota_ready, 1)
            pool.memset(ident[:], 0.0).then_inc(ident_zero, 1)
            pool.wait_ge(ident_zero, 1)
            pool.affine_select(out=ident[:], in_=ident[:], compare_op=ALU.not_equal, fill=1.0, base=0,
                               pattern=[[-1, P]], channel_multiplier=1).then_inc(ident_ready, 1)
            pool.wait_ge(rows_loaded, 16)
            for i, (norm_bias, bias) in enumerate((("ln1_b", "d2_b"), ("t_ln1_b", "f2_b"))):
                pool.tensor_tensor(bias_sum[:, i], row(norm_bias), row(bias), ALU.add).then_inc(bias_sums, 2)
            pool.wait_ge(second_loaded, SECOND)
            pool.tensor_tensor(w_rz[:], w_ih[:, :, 0:2 * H], w_hh[:, :, 0:2 * H], ALU.add).then_inc(rz_weights, 1)
            one = slice(0, 1)
            ih, hh = rows[one, slice(*span("b_ih"))], rows[one, slice(*span("b_hh"))]
            pool.tensor_tensor(b_gru[one, 0:2 * H], ih[:, 0:2 * H], hh[:, 0:2 * H], ALU.add).then_inc(bias_sums, 1)
            pool.tensor_copy(b_gru[one, 2 * H:3 * H], ih[:, 2 * H:3 * H]).then_inc(bias_sums, 1)
            pool.tensor_copy(b_gru[one, 3 * H:4 * H], hh[:, 2 * H:3 * H]).then_inc(bias_sums, 1)

        @block.scalar
        def _(act):
            act.dma_start(src_i[:], src_d).then_inc(idx_loaded, 16)
            act.dma_start(dst_i[:], dst_d).then_inc(idx_loaded, 16)
            act.dma_start(cols[:], cols_d).then_inc(cols_loaded, 16)
            act.dma_start(m2b[:].rearrange("p a f -> p (a f)"), m2b_d.to_broadcast([P, 2 * H])).then_inc(m2b_loaded, 16)
            for g, ws in enumerate(W):
                act.wait_ge(w_loaded[g], 16)
                nc.scalar.activation(w_hi[:, ws], w_raw[:, ws], ACT.Copy).then_inc(w_hi_done, 1)
                if g < 2:
                    act.wait_ge(x0_loaded[g], 16)
                    nc.scalar.activation(x_hi[:, 0, K_HALF[g]], x_raw[:, 0, K_HALF[g]], ACT.Copy).then_inc(x0_hi_done, 1)
            act.wait_ge(cols_loaded, 16)

            def edge(it):
                if it.has(1):
                    for h in range(2):
                        act.wait_ge(m2_biased, it.count(2, h - 1))
                        wait(act, lo2_done, it.count(2, h - 3))
                        nc.scalar.activation(m2[:, h], m2_in[:, h], ACT.Gelu)
                        wait(act, tile_summed, it.count(4, 2 * h - 6))
                        nc.scalar.activation(m2_hi[:, h], m2_in[:, h], ACT.Gelu).then_inc(gelu2, 1)
                if it.has():
                    for done, lo_done, read, out, out_hi, bank, bias, signal in (
                            (l0_done, lo0_done, l1_done, m0, m0_hi, bank0(it), "m0_b", gelu0),
                            (l1_done, lo1_done, l2_done, m1, m1_hi, bank1(it), "m1_b", gelu1)):
                        for m in range(KH):
                            act.wait_ge(done, it.count(2, m + 1))
                            wait(act, lo_done, it.count(2, m - 1))
                            nc.scalar.activation(out[:, m], ps[:, bank + m], ACT.Gelu, bias=col(bias, m))
                            wait(act, read, it.count(2, 0))
                            nc.scalar.activation(out_hi[:, m], ps[:, bank + m], ACT.Gelu,
                                                 bias=col(bias, m)).then_inc(signal, 1)
                if it.phase == 0 and it.has(1):
                    act.wait_ge(tile_summed, it.count(4, 0))
                    act.wait_ge(count_step, it.windows(8, -7))
                    for r in range(2):
                        nc.scalar.activation(packed[:, r], ps[:, CNT + r], ACT.Copy).then_inc(count_out, 1)

            iterations(act, edge)

            turned = [0]

            def affine(half, scale, bias):
                turned[0] += 1
                act.wait_ge(hat_turned, turned[0])
                for k in range(KH):
                    out, src = act_T[:, k, HALF[half]], turned_bank(half, k)
                    if scale:
                        nc.scalar.activation(out, src, ACT.Identity, bias=col(bias, k),
                                             scale=col(scale, k)).then_inc(act_ready, 1)
                    else:
                        nc.scalar.activation(out, src, ACT.Copy).then_inc(act_ready, 1)

            def round_d1w(m):
                if m >= 2:
                    act.wait_ge(d1_done, m - 1)
                nc.scalar.activation(d1w_hi[:, m % 2], d1_w[:, :, m * P:(m + 1) * P], ACT.Copy).then_inc(d1w_hi_done, 1)

            def gelu_split_out(i, out, bias, hi):
                if i >= 4:
                    act.wait_ge(gelu_split, i - 3)
                nc.scalar.activation(d_T[:, i % 4, 0:hi.shape[-1]], out, ACT.Gelu, bias=bias)
                nc.scalar.activation(hi, out, ACT.Gelu, bias=bias).then_inc(gelu_out, 1)

            act.wait_ge(early_loaded, 48)
            round_d1w(0)
            round_d1w(1)
            affine(0, "ln1_g", "ln1_b")
            for i in range(2 * KD):
                half, m = divmod(i, KD)
                if i == 2:
                    affine(1, "ln1_g", "ln1_b")
                act.wait_ge(d0_done, i + 1)
                gelu_split_out(i, ps[:, 4 + m % 4, 0:NH], col("d0_b", m), d0_hi[:, m, HALF[half]])
            for m in range(KD):
                act.wait_ge(d1_done, m + 1)
                gelu_split_out(2 * KD + m, ps[:, m % 4], col("d1_b", m), d1_hi[:, m])
                if m + 2 < KD:
                    round_d1w(m + 2)
                if m in (3, 4):
                    act.wait_ge(d2_loaded, 16)
                    ks = slice((m - 3) * 4, (m - 3) * 4 + 4)
                    nc.scalar.activation(d2w_hi[:, ks], d2_w[:, ks], ACT.Copy).then_inc(d2w_hi_done, 1)
            def qkv(c):
                act.wait_ge(qkv_done, c + 1)
                nc.scalar.activation(qk_rows[:, c], ps[:, c % 2], ACT.Copy).then_inc(qkv_out, 1)
                nc.scalar.activation(v_rows[:, c], ps[:, 4 + c % 2, 0:H], ACT.Copy).then_inc(qkv_out, 1)

            def exponential(c, at):
                act.wait_ge(scores_ready, at)
                nc.scalar.activation(probs[:, c], probs[:, c], ACT.Exp, scale=float(DH) ** -0.5).then_inc(exp_done, 1)

            def sums_out(c, at):
                act.wait_ge(prod_summed, at)
                nc.scalar.activation(x1[:, c], ps[:, OUT_BANK[c], 0:H], ACT.Copy).then_inc(x1_out, 1)

            affine(0, None, None)
            qkv(0)
            qkv(1)
            affine(1, None, None)
            exponential(0, 1)
            exponential(1, 2)
            qkv(2)
            qkv(3)
            sums_out(0, 3)
            exponential(3, 3)
            exponential(2, 4)
            sums_out(1, 5)
            sums_out(2, 6)
            act.wait_ge(bias_sums, 7)
            nc.scalar.activation(b_gru_hi[0:1], b_gru[0:1], ACT.Copy).then_inc(b_hi_done, 1)
            for half in range(2):
                affine(half, None, None)
            for half in range(2):
                affine(half, "t_ln1_w", "t_ln1_b")
                for pair in range(2):
                    act.wait_ge(f1_done, 2 * half + pair + 1)
                    for m in (2 * pair, 2 * pair + 1):
                        nc.scalar.activation(f1_T[:, m, HALF[half]], ps[:, pair, (m % 2) * NH:(m % 2 + 1) * NH], ACT.Relu,
                                             bias=col("f1_b", m)).then_inc(f1_relu, 1)
            affine(0, "t_ln2_w", "t_ln2_b")
            for c in range(NC):
                if c == 1:
                    affine(1, "t_ln2_w", "t_ln2_b")
                act.wait_ge(gru_done, c + 1)
                nc.scalar.activation(rz[:, c], ps[:, GRU_BANKS[c]], ACT.Sigmoid)
                nc.scalar.activation(one_less_z[:, c], ps[:, GRU_BANKS[c], H:2 * H], ACT.Sigmoid,
                                     scale=-1.0).then_inc(rz_sig, 1)
                if c:
                    act.wait_ge(cand_ready, c)
                    nc.scalar.activation(cand[:, c - 1], cand[:, c - 1], ACT.Tanh).then_inc(cand_tanh, 1)
            act.wait_ge(cand_ready, NC)
            nc.scalar.activation(cand[:, NC - 1], cand[:, NC - 1], ACT.Tanh).then_inc(cand_tanh, 1)

        @block.vector
        def _(dve):
            def split_x(par, landed, freed):
                dve.wait_ge(x_loaded[par], landed)
                wait(dve, l0_done, freed)
                nc.vector.tensor_copy(x_hi[:, par], x_raw[:, par]).then_inc(x_hi_done, 1)

            def rest_x(par, half, rounded, at):
                dve.wait_ge(rounded, at)
                ks = slice(2 * half, 2 * half + 2)
                nc.vector.tensor_tensor(x_lo[:, par, ks], x_raw[:, par, ks], x_hi[:, par, ks].bitcast(F32),
                                        ALU.subtract).then_inc(x_lo_done, 1)

            def rest_w(g):
                dve.wait_ge(w_hi_done, g + 1)
                nc.vector.tensor_tensor(w_lo[:, W[g]], w_raw[:, W[g]], w_hi[:, W[g]].bitcast(F32),
                                        ALU.subtract).then_inc(w_split, 1)

            for g in range(2):
                rest_w(g)
                rest_x(0, g, x0_hi_done, g + 1)
            rest_w(2)
            dve.wait_ge(idx_loaded, 32)
            dve.wait_ge(iota_ready, 1)
            nc.vector.tensor_copy(iota[:], iota_i[:]).then_inc(idx_step, 1)
            nc.vector.tensor_copy(dst_f[:], dst_i[:]).then_inc(idx_step, 1)
            nc.vector.tensor_copy(src_f[:], src_i[:]).then_inc(idx_step, 1)
            dve.wait_ge(idx_step, 3)
            nc.vector.tensor_scalar(src_far[:], src_f[:], float(N // 2), None, ALU.is_ge).then_inc(idx_step, 1)
            dve.wait_ge(idx_step, 4)
            nc.vector.scalar_tensor_tensor(src_in[:], src_far[:], -float(N // 2), src_f[:], ALU.mult,
                                           ALU.add).then_inc(idx_step, 1)
            nc.vector.tensor_scalar(src_unit[:], src_far[:], float((1 << PACK_BITS) - 1), 1.0, ALU.mult,
                                    ALU.add).then_inc(idx_step, 1)
            dve.wait_ge(idx_step, 6)
            rest_w(3)
            dve.wait_ge(m2b_loaded, 16)

            def hot(it, t):
                wait(dve, tile_summed, it.count(4, t - 7))
                at = bass.ds(it.count(4, t), 1)
                nc.vector.tensor_scalar(dst_hot[:, it.par, t], iota[:], dst_f[:, at], None, ALU.is_equal)
                nc.vector.tensor_scalar(pack_hot[:, it.par, t], iota[:, 0:2 * P], src_in[:, at], src_unit[:, at],
                                        ALU.is_equal, ALU.mult)
                nc.vector.tensor_scalar(src_hot[:, it.par, t], iota[:], src_f[:, at], None,
                                        ALU.is_equal).then_inc(hot_ready, 1)

            def rest(it, m, gelu, x, hi, lo, signal, back):
                dve.wait_ge(gelu, it.count(2, m + 1 - 2 * back))
                nc.vector.tensor_tensor(lo[:, m], x[:, m], hi[:, m].bitcast(F32), ALU.subtract).then_inc(signal, 1)

            def unpack(it, r):
                dve.wait_ge(count_out, it.windows(2, r - 1))
                dve.wait_ge(count_step, it.windows(8, 4 * r - 7))
                nc.vector.tensor_scalar(part[:, 0], packed[:, r], (1 << PACK_BITS) - 1, None,
                                        ALU.bitwise_and).then_inc(count_step, 1)
                nc.vector.tensor_scalar(part[:, 1], packed[:, r], PACK_BITS, None,
                                        ALU.logical_shift_right).then_inc(count_step, 1)
                for q in range(2):
                    dve.wait_ge(count_step, it.windows(8, 4 * r + q - 6))
                    s = 2 * q + r
                    nc.vector.tensor_tensor(count[:, s], count[:, s], part[:, q], ALU.add).then_inc(count_step, 1)

            def edge(it):
                nxt = 1 - it.par
                more = it.rnd is not None or it.b + 1 < NBLK
                counted = it.phase == 1 and (it.rnd is not None or it.b >= WINDOW)
                if it.has(1):
                    for h in range(2):
                        dve.wait_ge(l2_done, it.count(2, h - 1))
                        wait(dve, gelu2, it.count(2, h - 3))
                        nc.vector.tensor_tensor(m2_in[:, h], ps[:, (2 - bank0(it)) + h], m2b[:].rearrange("p a f -> p (a f)"),
                                                ALU.add).then_inc(m2_biased, 1)
                if more:
                    landed = 16 * ((it.b + 2) // 2)
                    if it.rnd is not None:
                        landed = it.rnd * (16 * WINDOW // 2) + landed
                    split_x(nxt, landed, it.count(2, 0))
                if it.has(1):
                    rest(it, 0, gelu2, m2, m2_hi, m2_lo, lo2_done, 1)
                if more:
                    rest_x(nxt, 0, x_hi_done, it.count(1, 1))
                if it.has(1):
                    rest(it, 1, gelu2, m2, m2_hi, m2_lo, lo2_done, 1)
                if it.has():
                    rest(it, 0, gelu0, m0, m0_hi, m0_lo, lo0_done, 0)
                    if more:
                        rest_x(nxt, 1, x_hi_done, it.count(1, 1))
                    hot(it, 0)
                    rest(it, 1, gelu0, m0, m0_hi, m0_lo, lo0_done, 0)
                    hot(it, 1)
                    if counted:
                        unpack(it, 0)
                    hot(it, 2)
                    rest(it, 0, gelu1, m1, m1_hi, m1_lo, lo1_done, 0)
                    hot(it, 3)
                    rest(it, 1, gelu1, m1, m1_hi, m1_lo, lo1_done, 0)
                if counted:
                    unpack(it, 1)

            iterations(dve, edge)

            steps = [0]

            def step(ins):
                steps[0] += 1
                ins.then_inc(dve_step, 1)
                return steps[0]

            def link(ins):
                dve.wait_ge(dve_step, step(ins))

            def moments(chunks):
                cs = slice(chunks[0], chunks[-1] + 1)
                for c in chunks:
                    ins = nc.vector.bn_aggr(mean_var[:, c], stats[:, c])
                link(ins)
                link(nc.vector.tensor_scalar(half_var[:, cs], mean_var[:, cs, 1], LN_EPS, 0.5, ALU.add, ALU.mult))
                link(nc.vector.tensor_scalar(rstd[:, cs].bitcast(I32), half_var[:, cs].bitcast(I32), -0.5,
                                             float(RSQRT_SEED), ALU.mult, ALU.add))
                for _ in range(3):
                    for c in chunks:
                        one = slice(c, c + 1)
                        ins = nc.vector.scalar_tensor_tensor(sq[:, one], rstd[:, one], half_var[:, one], rstd[:, one],
                                                             ALU.mult, ALU.mult)
                    link(ins)
                    link(nc.vector.scalar_tensor_tensor(rstd[:, cs], sq[:, cs], 1.5, rstd[:, cs], ALU.subtract, ALU.mult,
                                                        reverse0=True))

            def normed(src, out, c):
                return nc.vector.tensor_scalar(out[:, c], src[:, c], mean_var[:, c, 0:1], rstd[:, c:c + 1],
                                               ALU.subtract, ALU.mult)

            def sums_and_stats(chunks, done, product, add):
                written = []
                for c in chunks:
                    dve.wait_ge(done, c + 1)
                    written.append(step(nc.vector.tensor_tensor(res[:, c], product(c), add[:, c], ALU.add)))
                for c, at in zip(chunks, written):
                    dve.wait_ge(dve_step, at)
                    ins = nc.vector.bn_stats(stats[:, c], res[:, c])
                link(ins)

            def norm(half, done, product, add):
                sums_and_stats(CHUNKS[half], done, product, add)
                moments(CHUNKS[half])
                hats_written(half, lambda c: normed(res, hat, c))

            hats = [0]

            def hats_written(half, one):
                for c in CHUNKS[half]:
                    one(c).then_inc(hat_ready, 1)
                hats[0] += len(CHUNKS[half])

            def rows_after(half, weight, bias, add, hat_count):
                dve.wait_ge(hat_ready, hat_count)
                cs = slice(2 * half, 2 * half + 2)
                out = skip if add else h_rows
                link(nc.vector.tensor_tensor(out[:, cs], hat[:, cs], row_half(row(weight)), ALU.mult))
                nc.vector.tensor_tensor(out[:, cs], out[:, cs], row_half(add if add else row(bias)), ALU.add).then_inc(skip_ready, 1)
                skips[0] += 1

            skips = [0]

            def rest_d1w(m):
                dve.wait_ge(d1w_hi_done, m + 1)
                nc.vector.tensor_tensor(d1w_lo[:, m % 2], d1_w[:, :, m * P:(m + 1) * P], d1w_hi[:, m % 2].bitcast(F32),
                                        ALU.subtract).then_inc(d1w_split, 1)

            def rest_gelu(i, n, hi, lo):
                dve.wait_ge(gelu_out, i + 1)
                nc.vector.tensor_tensor(lo, d_T[:, i % 4, 0:n], hi.bitcast(F32), ALU.subtract).then_inc(gelu_split, 1)

            dve.wait_ge(tile_summed, E // P)
            for m in range(KH):
                nc.vector.tensor_scalar(sum_T[:, m], ps[:, SUM + m], 1.0 / 30.0, None, ALU.mult).then_inc(sum_scaled, 1)
            dve.wait_ge(early_loaded, 48)
            for half in range(2):
                norm(half, sum_turned, sum_rows, x_rows)
            for i in range(2 * KD):
                half, m = divmod(i, KD)
                rest_gelu(i, NH, d0_hi[:, m, HALF[half]], d0_lo[:, m, HALF[half]])
                if i in (4, 10):
                    rest_d1w(i // 10)
            for r in range(2):
                unpack(Iteration(NBLK), r)
            for m in range(KD):
                rest_gelu(2 * KD + m, N, d1_hi[:, m], d1_lo[:, m])
                if m + 2 < KD:
                    rest_d1w(m + 2)
                if m == 2:
                    dve.wait_ge(rows_loaded, 16)
                    dve.wait_ge(bias_sums, 4)
                    for half in range(2):
                        rows_after(half, "ln1_g", None, bias_row(0), hats[0])
                    link(nc.vector.tensor_tensor(skip2[:], x_rows[:], row_all("ln2_b"), ALU.add))
                if m in (3, 4):
                    dve.wait_ge(d2w_hi_done, m - 2)
                    ks = slice((m - 3) * 4, (m - 3) * 4 + 4)
                    nc.vector.tensor_tensor(d2w_lo[:, ks], d2_w[:, ks], d2w_hi[:, ks].bitcast(F32),
                                            ALU.subtract).then_inc(d2w_split, 1)
            dve.wait_ge(skip_ready, skips[0])

            def between_norms(chunks):
                marks = [step(nc.vector.scalar_tensor_tensor(res[:, c], res[:, c], mean_var[:, c, 0:1], row("ln2_g"),
                                                             ALU.subtract, ALU.mult)) for c in chunks]
                for i, c in enumerate(chunks):
                    dve.wait_ge(dve_step, marks[i])
                    marks[i] = step(nc.vector.scalar_tensor_tensor(res[:, c], res[:, c], rstd[:, c:c + 1], skip2[:, c],
                                                                   ALU.mult, ALU.add))
                for i, c in enumerate(chunks):
                    dve.wait_ge(dve_step, marks[i])
                    ins = nc.vector.bn_stats(stats[:, c], res[:, c])
                link(ins)

            sums_and_stats(CHUNKS[0], d2_done, product_rows, skip)
            moments(CHUNKS[0])
            between_norms(CHUNKS[0])
            sums_and_stats(CHUNKS[1], d2_done, product_rows, skip)
            moments(range(NC))
            hats_written(0, lambda c: normed(res, xp, c))
            between_norms(CHUNKS[1])
            moments(CHUNKS[1])
            hats_written(1, lambda c: normed(res, xp, c))
            pairs = [P, HEADS, HEADS, DH]

            def score_products(c):
                dve.wait_ge(qkv_out, 2 * c + 2)
                q = qk_rows[:, c, 0:H].rearrange("p (h a d) -> p h a d", h=HEADS, a=1).to_broadcast(pairs)
                k = qk_rows[:, c, H:2 * H].rearrange("p (a g d) -> p a g d", a=1, g=HEADS).to_broadcast(pairs)
                view = prod[c].rearrange("p (d h g) -> p h g d", h=HEADS, g=HEADS)
                return nc.vector.tensor_tensor(view, q, k, ALU.mult)

            def scores(c, at):
                dve.wait_ge(prod_summed, at)
                part_sums = ps[:, SCORE_BANK[c], 0:H].rearrange("p (d r) -> p r d", d=4)
                link(nc.vector.tensor_reduce(probs[:, c].rearrange("p h g -> p (h g)"), part_sums, AX_X, ALU.add))

            def each_g(t, c):
                return t[:, c * HEADS:(c + 1) * HEADS].rearrange("p (r a) -> p r a", a=1).to_broadcast([P, HEADS, HEADS])

            def less_top(c):
                link(nc.vector.tensor_reduce(top[:, c * HEADS:(c + 1) * HEADS], probs[:, c], AX_X, ALU.max))
                nc.vector.tensor_tensor(probs[:, c], probs[:, c], each_g(top, c), ALU.subtract).then_inc(scores_ready, 1)

            def softmax(c, at):
                dve.wait_ge(exp_done, at)
                one = slice(c * HEADS, (c + 1) * HEADS)
                link(nc.vector.tensor_reduce(total[:, one], probs[:, c], AX_X, ALU.add))
                link(nc.vector.reciprocal(total[:, one], total[:, one]))
                link(nc.vector.tensor_tensor(probs[:, c], probs[:, c], each_g(total, c), ALU.mult))

            def out_products(c):
                sm = probs[:, c].rearrange("p h (g a) -> p g h a", a=1).to_broadcast(pairs)
                v = v_rows[:, c].rearrange("p (g a d) -> p g a d", a=1, g=HEADS).to_broadcast(pairs)
                nc.vector.tensor_tensor(prod[c].rearrange("p (g h d) -> p g h d", h=HEADS, g=HEADS), sm, v,
                                        ALU.mult).then_inc(prod_ready, 1)

            score_products(0).then_inc(prod_ready, 1)
            score_products(1).then_inc(prod_ready, 1)
            for c in range(2):
                scores(c, c + 1)
                less_top(c)
                softmax(c, c + 1)
                if c == 0:
                    out_products(c)
                    nc.vector.tensor_tensor(skip[:, 0:2], xp[:, 0:2], row_half(row("O_b")), ALU.add)
            score_products(2).then_inc(prod_ready, 1)
            out_products(1)
            link(score_products(3))
            link(nc.vector.tensor_reduce(probs[:, 3].rearrange("p h g -> p (h g)"),
                                         prod[3].rearrange("p (d r) -> p r d", d=DH), AX_X, ALU.add))
            less_top(3)
            softmax(3, 3)
            scores(2, 4)
            less_top(2)
            softmax(2, 4)
            out_products(2)
            dve.wait_ge(hat_ready, hats[0])
            nc.vector.tensor_tensor(skip[:, 2:4], xp[:, 2:4], row_half(row("O_b")), ALU.add)
            sm = probs[:, 3].rearrange("p h (a g) -> p h a g", a=1).to_broadcast([P, HEADS, DH, HEADS])
            v = v_rows[:, 3].rearrange("p (a g d) -> p a d g", a=1, g=HEADS).to_broadcast([P, HEADS, DH, HEADS])
            view = prod[3].rearrange("p (h d g) -> p h d g", h=HEADS, d=DH)
            link(nc.vector.tensor_tensor(view, sm, v, ALU.mult))
            nc.vector.tensor_reduce(x1[:, 3].rearrange("p (h d) -> p h d", h=HEADS), view, AX_X,
                                    ALU.add).then_inc(x1_ready, 1)
            dve.wait_ge(x1_ready, 1)
            dve.wait_ge(x1_out, NC - 1)
            dve.wait_ge(b_hi_done, 1)
            nc.vector.tensor_scalar(ones[0:1], ident[0:1], 0.0, 1.0, ALU.mult, ALU.add)
            nc.vector.tensor_tensor(b_gru_lo[0:1], b_gru[0:1], b_gru_hi[0:1].bitcast(F32), ALU.subtract).then_inc(b_split, 1)
            for half in range(2):
                dve.wait_ge(gathered, half + 1)
                hats_written(half, lambda c: nc.vector.tensor_tensor(hat[:, c], x1[:, c], product_rows(c), ALU.mult))
            for half in range(2):
                norm(half, o_done, product_rows, skip)
                rows_after(half, "t_ln1_w", None, bias_row(1), hats[0])
            for half in range(2):
                dve.wait_ge(skip_ready, skips[0])
                norm(half, f2_done, product_rows, skip)
                rows_after(half, "t_ln2_w", "t_ln2_b", None, hats[0])
            dve.wait_ge(skip_ready, skips[0])

            def candidate_in(c):
                dve.wait_ge(rz_sig, c + 1)
                bank = GRU_BANKS[c] + 1
                at = step(nc.vector.tensor_tensor(cand[:, c], ps[:, bank, H:2 * H], rz[:, c, 0:H], ALU.mult))
                kept_at = step(nc.vector.tensor_tensor(kept[:, c], h_rows[:, c], rz[:, c, H:2 * H], ALU.mult))
                dve.wait_ge(dve_step, at)
                nc.vector.tensor_tensor(cand[:, c], cand[:, c], ps[:, bank, 0:H], ALU.add).then_inc(cand_ready, 1)
                dve.wait_ge(dve_step, kept_at)
                link(nc.vector.tensor_tensor(kept[:, c], kept[:, c], xp[:, c], ALU.add))

            def gru_out(c):
                dve.wait_ge(cand_tanh, c + 1)
                link(nc.vector.tensor_tensor(res[:, c], one_less_z[:, c], cand[:, c], ALU.mult))
                link(nc.vector.tensor_tensor(res[:, c], res[:, c], kept[:, c], ALU.add))
                step(nc.vector.bn_stats(stats[:, c], res[:, c]))

            def last_norm(half):
                dve.wait_ge(dve_step, steps[0])
                moments(CHUNKS[half])
                for c in CHUNKS[half]:
                    normed(res, hat, c).then_inc(out_ready, 1)

            for c in range(NC):
                candidate_in(c)
                if c >= 1:
                    gru_out(c - 1)
                if c == 2:
                    last_norm(0)
            gru_out(NC - 1)
            last_norm(1)

        @block.tensor
        def _(pe):
            def w(n, k, m, part):
                at = ((0, KE, KE + KH)[n] + k) * H
                return part[:, at + m * P:at + (m + 1) * P]

            def passes(a_hi, a_lo, b_hi, b_lo):
                return (a_hi, b_hi), (a_hi, b_lo), (a_lo, b_hi)

            def layer(it, n, bank, hi, lo, chunks, free, free_count, in_ready, in_count, done):
                for m in range(KH):
                    wait(pe, free, it.count(*free_count(m)))
                    for k in range(chunks):
                        if m == 0:
                            for s, value in in_ready(k):
                                pe.wait_ge(s, value)
                        ops = passes(w(n, k, m, w_hi), w(n, k, m, w_lo), hi[:, k], lo[:, k])
                        for i, (a, b) in enumerate(ops):
                            last = nc.tensor.matmul(ps[:, bank + m], a, b, start=(k == 0 and i == 0),
                                                    stop=(k == chunks - 1 and i == 2))
                    last.then_inc(done, 1)

            def sum_tile(it, t):
                par = 1 - it.par
                pe.wait_ge(hot_ready, it.count(4, t - 3))
                pe.wait_ge(lo2_done, it.count(2, t // 2 - 1))
                lone = it.rnd is None
                first, final = lone and it.b == 1 and t == 0, lone and it.b == NBLK and t == TB - 1
                phase = (it.phase - 1) % WINDOW
                if phase == 0 and t == 0 and not first:
                    pe.wait_ge(count_out, it.windows(2, 0))
                half, at = t // 2, (t % 2) * H
                for m in range(KH):
                    for i, part in enumerate((m2_hi, m2_lo)):
                        nc.tensor.matmul(ps[:, SUM + m], part[:, half, at + m * P:at + (m + 1) * P], src_hot[:, par, t],
                                         start=(first and i == 0), stop=(final and i == 1), skip_group_check=True)
                for r in range(2):
                    last = nc.tensor.matmul(ps[:, CNT + r], pack_hot[:, par, t, r * P:(r + 1) * P], dst_hot[:, par, t],
                                            start=(phase == 0 and t == 0), stop=(phase == WINDOW - 1 and t == TB - 1),
                                            skip_group_check=True)
                last.then_inc(tile_summed, 1)

            def messages(it):
                if it.first():
                    pe.wait_ge(w_split, 4)
                for t in range(TB):
                    h = t // 2
                    if t % 2 == 0:
                        pe.wait_ge(gelu0, it.count(2, h + 1))
                    if t == 0:
                        pe.wait_ge(lo1_done, it.count(2, 2))
                    out = ps[:, bank0(it) + h, (t % 2) * H:(t % 2 + 1) * H]
                    for k in range(KH):
                        e = slice(t * P, (t + 1) * P)
                        at = (KE + KH + k) * H
                        ops = passes(m1_hi[:, k, e], m1_lo[:, k, e], w_hi[:, at:at + H], w_lo[:, at:at + H])
                        for i, (a, b) in enumerate(ops):
                            last = nc.tensor.matmul(out, a, b, start=(k == 0 and i == 0), stop=(k == KH - 1 and i == 2))
                    if t % 2:
                        last.then_inc(l2_done, 1)

            def edge(it):
                if it.has():
                    layer(it, 0, bank0(it), x_hi[:, it.par], x_lo[:, it.par], KE, gelu1, lambda m: (2, m - 1),
                          lambda k: [(x_lo_done, it.count(2, k // 2 + 1))] * (k % 2 == 0)
                          + [(w_split, k // 2 + 1)] * (k % 2 == 0 and it.first()), None, l0_done)
                if it.has(1):
                    sum_tile(it, 0)
                    sum_tile(it, 1)
                if it.has():
                    if it.first():
                        pe.wait_ge(w_split, 3)
                    layer(it, 1, bank1(it), m0_hi, m0_lo, KH, m2_biased, lambda m: (2, m - 1),
                          lambda k: [(lo0_done, it.count(2, k + 1))], None, l1_done)
                if it.has(1):
                    sum_tile(it, 2)
                    sum_tile(it, 3)
                if it.has():
                    messages(it)

            def keep_warm(products, bank):
                for _ in range(products):
                    nc.tensor.matmul(ps[:, bank, 0:P], ident[:], ident[:], start=True, stop=True)

            pe.wait_ge(ident_ready, 1)
            keep_warm(16, 0)
            iterations(pe, edge)

            pe.wait_ge(sum_scaled, 2)
            pe.wait_ge(ident_ready, 1)
            for c in range(NC):
                if c == NC // 2:
                    pe.wait_ge(count_out, 2 * (NBLK // WINDOW))
                for m in range(KH):
                    last = nc.tensor.transpose(sum_rows(c)[:, m * P:(m + 1) * P], sum_T[:, m, c * P:(c + 1) * P], ident[:])
                last.then_inc(sum_turned, 1)
            keep_warm(10, 5)
            hats = [0]
            acts = [0]

            def turn_rows(src, half):
                for i, c in enumerate(CHUNKS[half]):
                    hats[0] += 1
                    pe.wait_ge(hat_ready, hats[0])
                    for k in range(KH):
                        last = nc.tensor.transpose(turned_bank(half, k)[:, i * P:(i + 1) * P], src[:, c, k * P:(k + 1) * P],
                                                   ident[:])
                last.then_inc(hat_turned, 1)
                acts[0] += KH
                return acts[0]

            def to_columns(weights, chunks, m, rhs, half, out):
                for k in range(chunks):
                    last = nc.tensor.matmul(out, weights[:, k, m * P:(m + 1) * P], rhs[:, k, HALF[half]], start=(k == 0),
                                            stop=(k == chunks - 1))
                return last

            def to_rows(lhs, chunks, weights, half, done):
                for c in CHUNKS[half]:
                    for k in range(chunks):
                        last = nc.tensor.matmul(product_rows(c), lhs[:, k, c * P:(c + 1) * P], weights[:, k],
                                                start=(k == 0), stop=(k == chunks - 1))
                    last.then_inc(done, 1)

            pe.wait_ge(early_loaded, 48)
            turned = [turn_rows(hat, 0), None]
            for i in range(2 * KD):
                half, m = divmod(i, KD)
                if i == 2:
                    turned[1] = turn_rows(hat, 1)
                if m == 0:
                    pe.wait_ge(act_ready, turned[half])
                if i >= 4:
                    pe.wait_ge(gelu_out, i - 3)
                to_columns(d0_w, KH, m, act_T, half, ps[:, 4 + m % 4, 0:NH]).then_inc(d0_done, 1)
            for m in range(KD):
                if m >= 4:
                    pe.wait_ge(gelu_out, 2 * KD + m - 3)
                pe.wait_ge(d1w_split, m + 1)
                for k in range(KD):
                    if m == 0:
                        pe.wait_ge(gelu_split, KD + k + 1)
                    ops = passes(d1w_hi[:, m % 2, k], d1w_lo[:, m % 2, k], d0_hi[:, k], d0_lo[:, k])
                    for i, (a, b) in enumerate(ops):
                        last = nc.tensor.matmul(ps[:, m % 4], a, b, start=(k == 0 and i == 0),
                                                stop=(k == KD - 1 and i == 2))
                last.then_inc(d1_done, 1)
            pe.wait_ge(d2w_split, 2)
            for c in range(NC):
                for k in range(KD):
                    if c == 0:
                        pe.wait_ge(gelu_split, 2 * KD + k + 1)
                    e = slice(c * P, (c + 1) * P)
                    ops = passes(d1_hi[:, k, e], d1_lo[:, k, e], d2w_hi[:, k], d2w_lo[:, k])
                    for i, (a, b) in enumerate(ops):
                        last = nc.tensor.matmul(product_rows(c), a, b, start=(k == 0 and i == 0),
                                                stop=(k == KD - 1 and i == 2))
                last.then_inc(d2_done, 1)
            keep_warm(14, 0)

            turned = [turn_rows(xp, 0), None]
            pe.wait_ge(second_loaded, SECOND)

            def qkv(c):
                pe.wait_ge(act_ready, turned[c // 2])
                if c >= 2:
                    pe.wait_ge(qkv_out, 2 * c - 2)
                for bank, weights, width in ((c % 2, wqk, 2 * H), (4 + c % 2, wv, H)):
                    for k in range(KH):
                        last = nc.tensor.matmul(ps[:, bank, 0:width], act_T[:, k, c * P:(c + 1) * P], weights[:, k],
                                                start=(k == 0), stop=(k == KH - 1))
                last.then_inc(qkv_done, 1)

            sums = [0]

            def add_up(c, bank):
                sums[0] += 1
                pe.wait_ge(prod_ready, sums[0])
                for j in range(HEADS):
                    last = nc.tensor.matmul(ps[:, bank, 0:H], ident[:], prod[c][:, j * H:(j + 1) * H],
                                            start=(j == 0), stop=(j == HEADS - 1))
                last.then_inc(prod_summed, 1)

            def gather(s):
                if s < NC - 1:
                    pe.wait_ge(x1_out, s + 1)
                else:
                    pe.wait_ge(x1_ready, 1)
                for c in range(NC):
                    last = nc.tensor.matmul(product_rows(c), count[:, s, c * P:(c + 1) * P], x1[:, s], start=(s == 0),
                                            stop=(s == NC - 1))
                    if s == NC - 1 and c % 2:
                        last.then_inc(gathered, 1)

            qkv(0)
            qkv(1)
            add_up(0, SCORE_BANK[0])
            turned[1] = turn_rows(xp, 1)
            add_up(1, SCORE_BANK[1])
            qkv(2)
            qkv(3)
            pe.wait_ge(qkv_out, 2 * NC)
            add_up(0, OUT_BANK[0])
            add_up(2, SCORE_BANK[2])
            add_up(1, OUT_BANK[1])
            pe.wait_ge(count_step, 1 + 8 * (NBLK // WINDOW))
            gather(0)
            add_up(2, OUT_BANK[2])
            for s in range(1, NC):
                gather(s)
            for half in range(2):
                pe.wait_ge(act_ready, turn_rows(hat, half))
                to_rows(act_T, KH, wo, half, o_done)
            turned = [turn_rows(hat, 0), None]
            for half in range(2):
                pe.wait_ge(act_ready, turned[half])
                for pair in range(2):
                    for m in (2 * pair, 2 * pair + 1):
                        last = to_columns(f1_w, KH, m, act_T, half, ps[:, pair, (m % 2) * NH:(m % 2 + 1) * NH])
                    last.then_inc(f1_done, 1)
                for c in CHUNKS[half]:
                    if c == 1:
                        turned[1] = turn_rows(hat, 1)
                    for k in range(4):
                        if c == CHUNKS[half][0]:
                            pe.wait_ge(f1_relu, 4 * half + k + 1)
                        last = nc.tensor.matmul(product_rows(c), f1_T[:, k, c * P:(c + 1) * P], f2_w[:, k],
                                                start=(k == 0), stop=(k == 3))
                    last.then_inc(f2_done, 1)
            pe.wait_ge(rz_weights, 1)
            pe.wait_ge(b_split, 1)
            turned = [turn_rows(hat, 0), None]
            for c in range(NC):
                if c == 1:
                    turned[1] = turn_rows(hat, 1)
                pe.wait_ge(act_ready, turned[c // 2])
                if GRU_BANKS[c] in GRU_BANKS[:c]:
                    before = GRU_BANKS.index(GRU_BANKS[c])
                    pe.wait_ge(rz_sig, before + 1)
                    pe.wait_ge(cand_ready, before + 1)
                bank = GRU_BANKS[c]
                for i, at in ((0, 0), (1, 2 * H)):
                    for part in (b_gru_hi, b_gru_lo):
                        nc.tensor.matmul(ps[:, bank + i], ones[0:1], part[0:1, at:at + 2 * H], start=(part is b_gru_hi),
                                         stop=False, skip_group_check=True)
                for k in range(KH):
                    nc.tensor.matmul(ps[:, bank], act_T[:, k, c * P:(c + 1) * P], w_rz[:, k], start=False,
                                     stop=(k == KH - 1), skip_group_check=True)
                for at, wn in ((0, w_ih), (H, w_hh)):
                    for k in range(KH):
                        last = nc.tensor.matmul(ps[:, bank + 1, at:at + H], act_T[:, k, c * P:(c + 1) * P],
                                                wn[:, k, 2 * H:3 * H], start=False, stop=(k == KH - 1),
                                                skip_group_check=True)
                last.then_inc(gru_done, 1)


def kernel(**inputs):
    import numpy as np
    import concourse.bacc as bacc
    from concourse.bass_utils import run_bass_kernel_spmd

    a = {k: np.asarray(v) for k, v in inputs.items()}

    def chunked(w):
        return np.ascontiguousarray(w.reshape(-1, P, w.shape[1]).transpose(1, 0, 2).reshape(P, -1))

    L0, L1 = "L0_gnn_", "L1_gnn_"
    col_src = {"m0_b": L0 + "m0_b", "m1_b": L0 + "m1_b", "ln1_g": L0 + "ln1_g", "ln1_b": L0 + "ln1_b",
               "d0_b": L0 + "d0_b", "d1_b": L0 + "d1_b", "t_ln1_w": L1 + "ln1_w", "t_ln1_b": L1 + "ln1_b",
               "f1_b": L1 + "f1_b", "t_ln2_w": L1 + "ln2_w", "t_ln2_b": L1 + "ln2_b"}
    row_src = {"ln1_g": L0 + "ln1_g", "ln1_b": L0 + "ln1_b", "d2_b": L0 + "d2_b", "ln2_g": L0 + "ln2_g",
               "ln2_b": L0 + "ln2_b", "O_b": L1 + "O_b", "t_ln1_w": L1 + "ln1_w", "t_ln1_b": L1 + "ln1_b",
               "f2_b": L1 + "f2_b", "t_ln2_w": L1 + "ln2_w", "t_ln2_b": L1 + "ln2_b", "b_ih": L1 + "gru_b_ih",
               "b_hh": L1 + "gru_b_hh"}
    data = [
        ("x_rows", chunked(a["x"])),
        ("edges", np.ascontiguousarray(a["edge_attr_512"].reshape(NBLK, BLK, KE, P).transpose(0, 3, 2, 1)
                                       .reshape(NBLK, P, KE * BLK))),
        ("src", np.ascontiguousarray(a["src"].reshape(E // P, P).T)),
        ("dst", np.ascontiguousarray(a["dst"].reshape(E // P, P).T)),
        ("w0", chunked(a[L0 + "m0_w"])), ("w1", chunked(a[L0 + "m1_w"])), ("w2", chunked(a[L0 + "m2_w"])),
        ("m2b", np.concatenate([a[L0 + "m2_b"]] * 2).reshape(1, 2 * H)),
        ("cols", np.ascontiguousarray(np.concatenate([a[col_src[n]].reshape(-1, P) for n in COLS]).T)),
        ("rows", np.concatenate([a[row_src[n]] for n in ROWS]).reshape(1, NROWS)),
        ("d0", chunked(a[L0 + "d0_w"])), ("d1", chunked(a[L0 + "d1_w"])), ("d2", chunked(a[L0 + "d2_w"])),
        ("wqk", chunked(np.concatenate([a[L1 + "Wq"], a[L1 + "Wk"]], axis=1))), ("wv", chunked(a[L1 + "Wv"])),
        ("wo", chunked(a[L1 + "O_w"])), ("f1", chunked(a[L1 + "f1_w"])), ("f2", chunked(a[L1 + "f2_w"])),
        ("wih", chunked(a[L1 + "gru_w_ih"])), ("whh", chunked(a[L1 + "gru_w_hh"])),
    ]
    nc = bacc.Bacc("TRN2", target_bir_lowering=False, num_devices=1)
    aps = [nc.dram_tensor(f"in_{n}_dram", v.shape, mybir.dt.from_np(v.dtype), kind="ExternalInput").ap() for n, v in data]
    out = nc.dram_tensor("out_dram", (NC, P, H), F32, kind="ExternalOutput").ap()
    gnn_kernel(nc, *aps, out)
    result = run_bass_kernel_spmd(nc, [{f"in_{n}_dram": v for n, v in data}], core_ids=[0])
    return result.results[0]["out_dram"].reshape(N, H)
```
